# Optimizing a Trainium2 kernel written in Bass

```python
import numpy as np
import jax
import jax.numpy as jnp

def _softmax(x, axis=-1):
    return jax.nn.softmax(x, axis=axis)

def _gelu(x):
    return jax.nn.gelu(x, approximate=True)

def _silu(x):
    return jax.nn.silu(x)

def _sigmoid(x):
    return jax.nn.sigmoid(x)

def _layernorm(x, axis=-1, eps=1e-05):
    m = jnp.mean(x, axis=axis, keepdims=True)
    v = jnp.var(x, axis=axis, keepdims=True)
    return (x - m) / jnp.sqrt(v + eps)

def _scatter_add(tgt, idx, src, axis=0):
    return tgt.at[idx].add(src)

def _segment_sum(src, seg, n):
    return jax.ops.segment_sum(src, seg, n)
kernel_name = 'mk_dlrm_tower_d1_rec_r8_807224'

def setup_inputs(seed: int=0):
    np.random.seed(seed)
    _w = jnp.asarray

    def _rec_inputs():
        import jax
        import jax.numpy as jnp
        _tk = jax.random.key(seed)
        dense_ctx = jax.random.normal(jax.random.fold_in(_tk, 190), (512, 16), jnp.float32)
        ids = jnp.stack([jax.random.randint(jax.random.fold_in(_tk, 200 + f), (512,), 0, v, jnp.int32) for f, v in enumerate([1000, 12500, 125000, 12500, 1000, 12500, 125000, 1250, 125000, 1250, 12500, 1250, 1250, 1000, 12500, 1250, 1000, 1250, 12500, 1000, 1000, 1250, 1250, 1250, 1250, 12500, 1250, 1250, 1250, 1250, 1250, 1250, 1250, 1250, 1000, 1000, 1000, 1000, 1250])], axis=1)
        tbl_0 = 0.05 * jax.random.normal(jax.random.fold_in(_tk, 500 + 0), (1000, 64), jnp.float32)
        tbl_1 = 0.05 * jax.random.normal(jax.random.fold_in(_tk, 500 + 1), (12500, 64), jnp.float32)
        tbl_2 = 0.05 * jax.random.normal(jax.random.fold_in(_tk, 500 + 2), (125000, 64), jnp.float32)
        tbl_3 = 0.05 * jax.random.normal(jax.random.fold_in(_tk, 500 + 3), (12500, 64), jnp.float32)
        tbl_4 = 0.05 * jax.random.normal(jax.random.fold_in(_tk, 500 + 4), (1000, 64), jnp.float32)
        tbl_5 = 0.05 * jax.random.normal(jax.random.fold_in(_tk, 500 + 5), (12500, 64), jnp.float32)
        tbl_6 = 0.05 * jax.random.normal(jax.random.fold_in(_tk, 500 + 6), (125000, 64), jnp.float32)
        tbl_7 = 0.05 * jax.random.normal(jax.random.fold_in(_tk, 500 + 7), (1250, 64), jnp.float32)
        tbl_8 = 0.05 * jax.random.normal(jax.random.fold_in(_tk, 500 + 8), (125000, 64), jnp.float32)
        tbl_9 = 0.05 * jax.random.normal(jax.random.fold_in(_tk, 500 + 9), (1250, 64), jnp.float32)
        tbl_10 = 0.05 * jax.random.normal(jax.random.fold_in(_tk, 500 + 10), (12500, 64), jnp.float32)
        tbl_11 = 0.05 * jax.random.normal(jax.random.fold_in(_tk, 500 + 11), (1250, 64), jnp.float32)
        tbl_12 = 0.05 * jax.random.normal(jax.random.fold_in(_tk, 500 + 12), (1250, 64), jnp.float32)
        tbl_13 = 0.05 * jax.random.normal(jax.random.fold_in(_tk, 500 + 13), (1000, 64), jnp.float32)
        tbl_14 = 0.05 * jax.random.normal(jax.random.fold_in(_tk, 500 + 14), (12500, 64), jnp.float32)
        tbl_15 = 0.05 * jax.random.normal(jax.random.fold_in(_tk, 500 + 15), (1250, 64), jnp.float32)
        tbl_16 = 0.05 * jax.random.normal(jax.random.fold_in(_tk, 500 + 16), (1000, 64), jnp.float32)
        tbl_17 = 0.05 * jax.random.normal(jax.random.fold_in(_tk, 500 + 17), (1250, 64), jnp.float32)
        tbl_18 = 0.05 * jax.random.normal(jax.random.fold_in(_tk, 500 + 18), (12500, 64), jnp.float32)
        tbl_19 = 0.05 * jax.random.normal(jax.random.fold_in(_tk, 500 + 19), (1000, 64), jnp.float32)
        tbl_20 = 0.05 * jax.random.normal(jax.random.fold_in(_tk, 500 + 20), (1000, 64), jnp.float32)
        tbl_21 = 0.05 * jax.random.normal(jax.random.fold_in(_tk, 500 + 21), (1250, 64), jnp.float32)
        tbl_22 = 0.05 * jax.random.normal(jax.random.fold_in(_tk, 500 + 22), (1250, 64), jnp.float32)
        tbl_23 = 0.05 * jax.random.normal(jax.random.fold_in(_tk, 500 + 23), (1250, 64), jnp.float32)
        tbl_24 = 0.05 * jax.random.normal(jax.random.fold_in(_tk, 500 + 24), (1250, 64), jnp.float32)
        tbl_25 = 0.05 * jax.random.normal(jax.random.fold_in(_tk, 500 + 25), (12500, 64), jnp.float32)
        tbl_26 = 0.05 * jax.random.normal(jax.random.fold_in(_tk, 500 + 26), (1250, 64), jnp.float32)
        tbl_27 = 0.05 * jax.random.normal(jax.random.fold_in(_tk, 500 + 27), (1250, 64), jnp.float32)
        tbl_28 = 0.05 * jax.random.normal(jax.random.fold_in(_tk, 500 + 28), (1250, 64), jnp.float32)
        tbl_29 = 0.05 * jax.random.normal(jax.random.fold_in(_tk, 500 + 29), (1250, 64), jnp.float32)
        tbl_30 = 0.05 * jax.random.normal(jax.random.fold_in(_tk, 500 + 30), (1250, 64), jnp.float32)
        tbl_31 = 0.05 * jax.random.normal(jax.random.fold_in(_tk, 500 + 31), (1250, 64), jnp.float32)
        tbl_32 = 0.05 * jax.random.normal(jax.random.fold_in(_tk, 500 + 32), (1250, 64), jnp.float32)
        tbl_33 = 0.05 * jax.random.normal(jax.random.fold_in(_tk, 500 + 33), (1250, 64), jnp.float32)
        tbl_34 = 0.05 * jax.random.normal(jax.random.fold_in(_tk, 500 + 34), (1000, 64), jnp.float32)
        tbl_35 = 0.05 * jax.random.normal(jax.random.fold_in(_tk, 500 + 35), (1000, 64), jnp.float32)
        tbl_36 = 0.05 * jax.random.normal(jax.random.fold_in(_tk, 500 + 36), (1000, 64), jnp.float32)
        tbl_37 = 0.05 * jax.random.normal(jax.random.fold_in(_tk, 500 + 37), (1000, 64), jnp.float32)
        tbl_38 = 0.05 * jax.random.normal(jax.random.fold_in(_tk, 500 + 38), (1250, 64), jnp.float32)
        _rk = jax.random.fold_in(_tk, 7)
        W_top1 = 0.0363456 * jax.random.normal(jax.random.fold_in(_tk, 801), (757, 512), jnp.float32)
        W_top2 = 0.0441942 * jax.random.normal(jax.random.fold_in(_tk, 802), (512, 256), jnp.float32)
        W_top3 = 0.0625 * jax.random.normal(jax.random.fold_in(_tk, 803), (256, 1), jnp.float32)
        b_top1 = jnp.zeros((512,), jnp.float32)
        b_top2 = jnp.zeros((256,), jnp.float32)
        return (dense_ctx, ids, tbl_0, tbl_1, tbl_2, tbl_3, tbl_4, tbl_5, tbl_6, tbl_7, tbl_8, tbl_9, tbl_10, tbl_11, tbl_12, tbl_13, tbl_14, tbl_15, tbl_16, tbl_17, tbl_18, tbl_19, tbl_20, tbl_21, tbl_22, tbl_23, tbl_24, tbl_25, tbl_26, tbl_27, tbl_28, tbl_29, tbl_30, tbl_31, tbl_32, tbl_33, tbl_34, tbl_35, tbl_36, tbl_37, tbl_38, W_top1, b_top1, W_top2, b_top2, W_top3)
    dense_ctx, ids, tbl_0, tbl_1, tbl_2, tbl_3, tbl_4, tbl_5, tbl_6, tbl_7, tbl_8, tbl_9, tbl_10, tbl_11, tbl_12, tbl_13, tbl_14, tbl_15, tbl_16, tbl_17, tbl_18, tbl_19, tbl_20, tbl_21, tbl_22, tbl_23, tbl_24, tbl_25, tbl_26, tbl_27, tbl_28, tbl_29, tbl_30, tbl_31, tbl_32, tbl_33, tbl_34, tbl_35, tbl_36, tbl_37, tbl_38, W_top1, b_top1, W_top2, b_top2, W_top3 = _rec_inputs()

    def _L0_rec_setup():
        import jax, jax.numpy as jnp
        import numpy as np
        NUM_FIELDS = 39
        _ROW, _COL = np.triu_indices(NUM_FIELDS, k=1)
        key = jax.random.key(seed)
        x = jax.random.normal(key, (2048, NUM_FIELDS, 64), dtype=jnp.float32)
        return {'x': x}
    _L0_rec_all = _L0_rec_setup()
    _L0_rec_in = {k: v for k, v in _L0_rec_all.items() if k in ()}
    del _L0_rec_all
    return {'dense_ctx': dense_ctx, 'ids': ids, 'tbl_0': tbl_0, 'tbl_1': tbl_1, 'tbl_2': tbl_2, 'tbl_3': tbl_3, 'tbl_4': tbl_4, 'tbl_5': tbl_5, 'tbl_6': tbl_6, 'tbl_7': tbl_7, 'tbl_8': tbl_8, 'tbl_9': tbl_9, 'tbl_10': tbl_10, 'tbl_11': tbl_11, 'tbl_12': tbl_12, 'tbl_13': tbl_13, 'tbl_14': tbl_14, 'tbl_15': tbl_15, 'tbl_16': tbl_16, 'tbl_17': tbl_17, 'tbl_18': tbl_18, 'tbl_19': tbl_19, 'tbl_20': tbl_20, 'tbl_21': tbl_21, 'tbl_22': tbl_22, 'tbl_23': tbl_23, 'tbl_24': tbl_24, 'tbl_25': tbl_25, 'tbl_26': tbl_26, 'tbl_27': tbl_27, 'tbl_28': tbl_28, 'tbl_29': tbl_29, 'tbl_30': tbl_30, 'tbl_31': tbl_31, 'tbl_32': tbl_32, 'tbl_33': tbl_33, 'tbl_34': tbl_34, 'tbl_35': tbl_35, 'tbl_36': tbl_36, 'tbl_37': tbl_37, 'tbl_38': tbl_38, 'W_top1': W_top1, 'b_top1': b_top1, 'W_top2': W_top2, 'b_top2': b_top2, 'W_top3': W_top3}

def reference(dense_ctx, ids, tbl_0, tbl_1, tbl_2, tbl_3, tbl_4, tbl_5, tbl_6, tbl_7, tbl_8, tbl_9, tbl_10, tbl_11, tbl_12, tbl_13, tbl_14, tbl_15, tbl_16, tbl_17, tbl_18, tbl_19, tbl_20, tbl_21, tbl_22, tbl_23, tbl_24, tbl_25, tbl_26, tbl_27, tbl_28, tbl_29, tbl_30, tbl_31, tbl_32, tbl_33, tbl_34, tbl_35, tbl_36, tbl_37, tbl_38, W_top1, b_top1, W_top2, b_top2, W_top3):
    import jax
    import jax.numpy as jnp

    def _L0_rec_ref(x):
        import jax, jax.numpy as jnp
        import numpy as np
        NUM_FIELDS = 39
        _ROW, _COL = np.triu_indices(NUM_FIELDS, k=1)
        s = jnp.sum(x, axis=-1)
        return s[:, _ROW] * s[:, _COL]
    e = jnp.stack([tbl_0[ids[:, 0]], tbl_1[ids[:, 1]], tbl_2[ids[:, 2]], tbl_3[ids[:, 3]], tbl_4[ids[:, 4]], tbl_5[ids[:, 5]], tbl_6[ids[:, 6]], tbl_7[ids[:, 7]], tbl_8[ids[:, 8]], tbl_9[ids[:, 9]], tbl_10[ids[:, 10]], tbl_11[ids[:, 11]], tbl_12[ids[:, 12]], tbl_13[ids[:, 13]], tbl_14[ids[:, 14]], tbl_15[ids[:, 15]], tbl_16[ids[:, 16]], tbl_17[ids[:, 17]], tbl_18[ids[:, 18]], tbl_19[ids[:, 19]], tbl_20[ids[:, 20]], tbl_21[ids[:, 21]], tbl_22[ids[:, 22]], tbl_23[ids[:, 23]], tbl_24[ids[:, 24]], tbl_25[ids[:, 25]], tbl_26[ids[:, 26]], tbl_27[ids[:, 27]], tbl_28[ids[:, 28]], tbl_29[ids[:, 29]], tbl_30[ids[:, 30]], tbl_31[ids[:, 31]], tbl_32[ids[:, 32]], tbl_33[ids[:, 33]], tbl_34[ids[:, 34]], tbl_35[ids[:, 35]], tbl_36[ids[:, 36]], tbl_37[ids[:, 37]], tbl_38[ids[:, 38]]], axis=1)
    z = _L0_rec_ref(e)
    z = z.reshape(z.shape[0], -1)
    h = jnp.concatenate([z, dense_ctx], axis=1)
    h = jnp.maximum(h @ W_top1 + b_top1, 0.0)
    h = jnp.maximum(h @ W_top2 + b_top2, 0.0)
    y = h @ W_top3
    return y

_drawn_inputs = setup_inputs


def setup_inputs(seed=0):
    import zlib

    import numpy as np

    out = dict(_drawn_inputs(seed))
    spreads = {'b_top1': (0.0, 0.1), 'b_top2': (0.0, 0.1)}
    factors = {}
    for name, (base, spread) in spreads.items():
        noise = np.random.default_rng([zlib.crc32(name.encode()), seed]).standard_normal(out[name].shape)
        drawn = base * np.exp(spread * noise) if base else spread * noise
        out[name] = jnp.asarray(drawn.astype(out[name].dtype))
    for name, factor in factors.items():
        out[name] = (out[name] * factor).astype(out[name].dtype)
    return out
```

```python
from contextlib import ExitStack

import numpy as np
import concourse.bass as bass
from concourse import mybir

P = 128
B = 512
D = 64
FIELDS = 39
DENSE = 16
PARTS = 3
SMALL_ROWS = 1280
CMAX = SMALL_ROWS // P
N1, N2 = 512, 256
NB1, NB2 = N1 // P, N2 // P
TILES = B // P
GROUP = 4
QUAD = 32
assert PARTS * CMAX <= QUAD

RANGES = [(0, 384), (384, 512)]


def plan(rows):
    small = sorted((f for f in range(FIELDS) if rows[f] <= SMALL_ROWS), key=lambda f: (-rows[f], f))
    big = [f for f in range(FIELDS) if rows[f] > SMALL_ROWS]
    cols = [-(-rows[f] // P) for f in small]
    groups = []
    at = 0
    while at < len(small):
        n = 1
        while n < GROUP and at + n < len(small) and cols[at + n] == cols[at]:
            n += 1
        groups.append((at, n, cols[at]))
        at += n
    ns, nb = len(small), len(big)
    ss = [(("s", i), ("s", j)) for j in range(ns) for i in range(j)]
    sb = [(("s", i), ("b", j)) for j in range(nb) for i in range(ns)]
    bb = [(("b", i), ("b", j)) for j in range(nb) for i in range(j)]
    pairs = ss + sb + bb
    sizes = [120, P, P, P, P]
    sizes.append(len(pairs) - sum(sizes))
    chunks, at = [], 0
    for n in sizes:
        chunks.append(pairs[at:at + n])
        at += n
    return small, big, cols, groups, chunks


def after_group(groups, chunk):
    last = max(j for _, (_, j) in chunk)
    return next(g for g, (f0, n, _) in enumerate(groups) if last < f0 + n)


def selectors(chunks, ns, nb):
    use = []
    for c, chunk in enumerate(chunks):
        for side in (0, 1):
            for kind in "sb":
                if any(pair[side][0] == kind for pair in chunk):
                    use.append((c, side, kind))
    return use


def build(nc, rows, idx_big, ids_small, tables, big_tables, dense, w1, w2, vectors, ident_c, group_c, select_c, out):
    f32, bf16, i32 = mybir.dt.float32, mybir.dt.bfloat16, mybir.dt.int32
    ALU = mybir.AluOpType
    ACT = mybir.ActivationFunctionType
    AX = mybir.AxisListType

    small, big, cols, groups, chunks = plan(rows)
    NS, NBIG, NG, NCH = len(small), len(big), len(groups), len(chunks)
    KS, KB = PARTS * NS, PARTS * NBIG
    col0 = [sum(cols[:f]) for f in range(NS + 1)]
    uses = selectors(chunks, NS, NBIG)
    early = [c for c in range(NCH) if all(b[0] == "s" for _, b in chunks[c])]
    late = [c for c in range(NCH) if c not in early]
    snap_after = [after_group(groups, chunks[c]) for c in early]
    snap_after[-1] = NG - 1
    NP5 = len(chunks[-1])
    V_P, V_C, V_B1, V_B2, V_W3 = 0, 1, 2, 2 + NB1, 2 + NB1 + NB2

    with ExitStack() as ctx:
        def sb(name, shape, dt):
            return ctx.enter_context(nc.sbuf_tensor(name, shape, dt))

        def sem(name):
            return ctx.enter_context(nc.semaphore(name))

        table = sb("table", [P, col0[NS] * D], f32)
        row_sum = sb("row_sum", [P, col0[NS]], f32)
        rest = sb("rest", [P, 2, GROUP * CMAX], f32)
        parts = sb("parts", [P, NS, QUAD], bf16)
        ids_s = sb("ids_s", [NS, B], i32)
        row_i = sb("row_i", [NS, B], i32)
        col_i = sb("col_i", [NS, B], i32)
        row_b = sb("row_b", [NS, B], bf16)
        col_b = sb("col_b", [NS, B], bf16)
        row_all = sb("row_all", [P, 2, GROUP, B], bf16)
        col_all = sb("col_all", [P, 2, B], bf16)
        onehot = sb("onehot", [P, NS, B], bf16)
        col_mask = sb("col_mask", [P, NG, B], bf16)
        masked = sb("masked", [P, 2, B], bf16)
        stack_s = sb("stack_s", [KS, B], bf16)
        idx = sb("idx", [P, TILES * NBIG], i32)
        rows_b = sb("rows_b", [P, TILES, NBIG, D], f32)
        junk = sb("junk", [P, TILES, NBIG, D], f32)
        sum_b = sb("sum_b", [P, TILES, NBIG], f32)
        rest_b = sb("rest_b", [P, TILES, NBIG], f32)
        parts_b = sb("parts_b", [P, TILES, PARTS, NBIG], bf16)
        stack_b = sb("stack_b", [KB, B], bf16)
        factor = sb("factor", [P, 2, B], f32)
        z = sb("z", [P, NCH, B], f32)
        w1_s = sb("w1_s", [P, NCH, N1], f32)
        w2_s = sb("w2_s", [P, NB1, N2], f32)
        vec = sb("vec", [P, V_W3 + NB2], f32)
        ident = sb("ident", [P, P], bf16)
        group_rows = sb("group_rows", [NS, NG * P], bf16)
        select = sb("select", [P, NG * KS + len(uses) * P], bf16)
        h1 = sb("h1", [P, NB1, B], f32)
        h2 = sb("h2", [P, NB2, B], f32)
        y = sb("y", [1, B], f32)

        bank = [ctx.enter_context(nc.psum_tensor(f"bank{i}", [P, 2, B], f32)) for i in range(2)]
        low = [bank[0][:, 0, :], bank[0][:, 1, :], bank[1][:, 0, :], bank[1][:, 1, :]]
        high = [ctx.enter_context(nc.psum_tensor(f"bank{i}", [P, B], f32)) for i in range(4, 8)]
        PICK, STACK = high[0], high[2]
        SEL_A, SEL_B = high[1], high[3]

        def gather_sum(g):
            return select[:, g * KS:(g + 1) * KS]

        def selector(c, side, kind):
            u = uses.index((c, side, kind))
            k, m = (KS if kind == "s" else KB), len(chunks[c])
            return select[0:k, NG * KS + u * P:NG * KS + u * P + m]

        ids_in, idx_in, ident_in, vec_in, group_in = (
            sem("ids_in"), sem("idx_in"), sem("ident_in"), sem("vec_in"), sem("group_in"))
        select_in, dense_in, w1_in, w2_in = sem("select_in"), sem("dense_in"), sem("w1_in"), sem("w2_in")
        table_in = [sem(f"table_in{g}") for g in range(NG)]
        gathered = [sem(f"gathered{t}") for t in range(TILES)]
        out_written = sem("out_written")
        parts_zeroed = sem("parts_zeroed")
        ids_cut, ids_cut_b = sem("ids_cut"), sem("ids_cut_b")
        row_spread, row_copied = sem("row_spread"), sem("row_copied")
        col_spread, col_copied = sem("col_spread"), sem("col_copied")
        onehot_made, mask_made = sem("onehot_made"), sem("mask_made")
        rows_summed, high_made, rest_made, mid_made, parts_made = (
            sem("rows_summed"), sem("high_made"), sem("rest_made"), sem("mid_made"), sem("parts_made"))
        picked, masked_made, stacked, snapped = sem("picked"), sem("masked_made"), sem("stacked"), sem("snapped")
        big_summed, big_high, big_rest, big_mid, big_parts = (
            sem("big_summed"), sem("big_high"), sem("big_rest"), sem("big_mid"), sem("big_parts"))
        big_turned, big_stacked = sem("big_turned"), sem("big_stacked")
        selected, factor_copied, z_made = sem("selected"), sem("factor_copied"), sem("z_made")
        l1_done, h1_made, l2_done, h2_made, l3_done, y_made = (
            sem("l1_done"), sem("h1_made"), sem("l2_done"), sem("h2_made"), sem("l3_done"), sem("y_made"))

        def sel_banks(k):
            if k < len(early) or (k - len(early)) % len(late) % 2 == 1:
                return SEL_A, SEL_B
            return PICK, STACK

        halves = [0]
        for _, n, _ in groups:
            halves.append(halves[-1] + -(-n // 2))

        block = ctx.enter_context(nc.Block())

        @block.sync
        def _(sp):
            def load_table(g):
                f0, n, c = groups[g]
                a, b = col0[f0] * D, col0[f0 + n] * D
                sp.dma_start(table[:, a:b], tables[:, a:b]).then_inc(table_in[g], 16)

            sp.dma_start(ids_s[:, :], ids_small).then_inc(ids_in, 16)
            load_table(0)
            sp.dma_start(vec[:, :], vectors).then_inc(vec_in, 16)
            load_table(1)
            sp.dma_start(select[:, :], select_c).then_inc(select_in, 16)
            for g in range(2, NG):
                load_table(g)
                if g == 3:
                    sp.dma_start(w1_s[:, :, :], w1).then_inc(w1_in, 16)
                    sp.dma_start(z[NP5:NP5 + DENSE, NCH - 1, :], dense).then_inc(dense_in, 16)
            sp.dma_start(w2_s[:, :, :], w2).then_inc(w2_in, 16)
            sp.wait_ge(y_made, len(RANGES))
            sp.dma_start(out.rearrange("b one -> one b"), y[:, :]).then_inc(out_written, 16)
            sp.wait_ge(out_written, 16)

        @block.gpsimd
        def _(pool):
            pool.wait_ge(idx_in, 16)
            for t in range(TILES):
                for f in range(NBIG):
                    k = t * NBIG + f
                    nc.gpsimd.indirect_dma_start(
                        rows_b[:, t, f, :], None, big_tables[f],
                        bass.IndirectOffsetOnAxis(ap=idx[:, k:k + 1], axis=0)).then_inc(gathered[t], 16)

        @block.scalar
        def _(act):
            act.dma_start(idx[:, :], idx_big).then_inc(idx_in, 16)
            act.dma_start(ident[:, :], ident_c).then_inc(ident_in, 16)
            act.dma_start(group_rows[:, :], group_c).then_inc(group_in, 16)

            def copy_spread(g):
                _, n, _ = groups[g]
                if g >= 2:
                    act.wait_ge(onehot_made, g - 1)
                for h in range(2):
                    m = min(2, n - 2 * h)
                    if m > 0:
                        act.wait_ge(row_spread, halves[g] + h + 1)
                        nc.scalar.copy(row_all[:, g % 2, 2 * h:2 * h + m, :], bank[h][:, 0:m, :]).then_inc(row_copied, 1)
                act.wait_ge(col_spread, g + 1)
                if g >= 2:
                    act.wait_ge(mask_made, g - 1)
                q = n * QUAD
                nc.scalar.copy(col_all[0:q, g % 2, :], (SEL_A, SEL_B)[g % 2][0:q, :]).then_inc(col_copied, 1)

            def snap(s):
                act.wait_ge(stacked, snap_after[s] + 1)
                if s >= 1:
                    act.wait_ge(selected, s)
                nc.scalar.copy(stack_s[:, :], STACK[0:KS, :]).then_inc(snapped, 1)

            def sum_big(t):
                act.wait_ge(gathered[t], 16 * NBIG)
                for f in range(NBIG):
                    i = nc.scalar.activation(junk[:, t, f, :], rows_b[:, t, f, :], ACT.Copy,
                                             accum_out=sum_b[:, t, f:f + 1])
                i.then_inc(big_summed, 1)

            def copy_factor(k, c, a, b):
                m = len(chunks[c])
                act.wait_ge(selected, k + 1)
                if k >= 2:
                    act.wait_ge(z_made, k - 1)
                nc.scalar.copy(factor[0:m, k % 2, a:b], sel_banks(k)[0][0:m, a:b]).then_inc(factor_copied, 1)

            for g in range(NG):
                copy_spread(g)
            for s, c in enumerate(early):
                snap(s)
                if s + 1 < len(early):
                    copy_factor(s, c, 0, B)
                sum_big(s)
            copy_factor(len(early) - 1, early[-1], 0, B)
            act.wait_ge(vec_in, 16)
            for r, (a, b) in enumerate(RANGES):
                act.wait_ge(big_turned, r + 1)
                nc.scalar.copy(stack_b[:, a:b], STACK[0:KB, a:b] if r == 0 else SEL_B[0:KB, a:b]).then_inc(big_stacked, 1)
                for i, c in enumerate(late):
                    copy_factor(len(early) + r * len(late) + i, c, a, b)
                for n in range(NB1):
                    act.wait_ge(l1_done, r * NB1 + n + 1)
                    nc.scalar.activation(h1[:, n, a:b], low[n][:, a:b], ACT.Relu,
                                         bias=vec[:, V_B1 + n:V_B1 + n + 1]).then_inc(h1_made, 1)
                for m in range(NB2):
                    act.wait_ge(l2_done, r * NB2 + m + 1)
                    nc.scalar.activation(h2[:, m, a:b], (PICK, STACK)[m][:, a:b], ACT.Relu,
                                         bias=vec[:, V_B2 + m:V_B2 + m + 1]).then_inc(h2_made, 1)
                act.wait_ge(l3_done, r + 1)
                nc.scalar.copy(y[:, a:b], SEL_A[0:1, a:b]).then_inc(y_made, 1)

        @block.vector
        def _(dve):
            nc.vector.memset(parts[:, :, :], 0.0).then_inc(parts_zeroed, 1)
            dve.wait_ge(ids_in, 16)
            nc.vector.tensor_single_scalar(row_i[:, :], ids_s[:, :], P - 1, ALU.bitwise_and).then_inc(ids_cut, 1)
            nc.vector.tensor_single_scalar(col_i[:, :], ids_s[:, :], 7, ALU.logical_shift_right).then_inc(ids_cut, 1)
            dve.wait_ge(ids_cut, 1)
            nc.vector.tensor_copy(row_b[:, :], row_i[:, :]).then_inc(ids_cut_b, 1)
            dve.wait_ge(ids_cut, 2)
            nc.vector.tensor_copy(col_b[:, :], col_i[:, :]).then_inc(ids_cut_b, 1)
            dve.wait_ge(vec_in, 16)

            def make_masks(g):
                f0, n, _ = groups[g]
                q = n * QUAD
                dve.wait_ge(row_copied, halves[g + 1])
                nc.vector.tensor_scalar(onehot[:, f0:f0 + n, :], row_all[:, g % 2, 0:n, :], vec[:, V_P:V_P + 1],
                                        None, ALU.is_equal).then_inc(onehot_made, 1)
                dve.wait_ge(col_copied, g + 1)
                nc.vector.tensor_scalar(col_mask[0:q, g, :], col_all[0:q, g % 2, :], vec[0:q, V_C:V_C + 1],
                                        None, ALU.is_equal).then_inc(mask_made, 1)

            def sum_rows(g):
                f0, n, c = groups[g]
                a, b = col0[f0], col0[f0 + n]
                dve.wait_ge(table_in[g], 16)
                nc.vector.tensor_reduce(row_sum[:, a:b], table[:, a * D:b * D].rearrange("p (r d) -> p r d", d=D),
                                        AX.X, ALU.add).then_inc(rows_summed, 1)

            def split_sums(g):
                f0, n, c = groups[g]
                s = row_sum[:, col0[f0]:col0[f0 + n]].rearrange("p (f c) -> p f c", c=c)
                part = [parts[:, f0:f0 + n, k * CMAX:k * CMAX + c] for k in range(PARTS)]
                r = [rest[:, k, 0:n * c].rearrange("p (f c) -> p f c", c=c) for k in range(2)]
                dve.wait_ge(rows_summed, g + 1)
                if g == 0:
                    dve.wait_ge(parts_zeroed, 1)
                nc.vector.tensor_copy(part[0], s).then_inc(high_made, 1)
                dve.wait_ge(high_made, g + 1)
                nc.vector.tensor_tensor(r[0], s, part[0], ALU.subtract).then_inc(rest_made, 1)
                dve.wait_ge(rest_made, g + 1)
                nc.vector.tensor_copy(part[1], r[0]).then_inc(mid_made, 1)
                dve.wait_ge(mid_made, g + 1)
                nc.vector.tensor_tensor(part[2], r[0], part[1], ALU.subtract).then_inc(parts_made, 1)

            def mask_picked(g):
                q = groups[g][1] * QUAD
                dve.wait_ge(mask_made, g + 1)
                dve.wait_ge(picked, g + 1)
                if g >= 2:
                    dve.wait_ge(stacked, g - 1)
                nc.vector.tensor_tensor(masked[0:q, g % 2, :], PICK[0:q, :], col_mask[0:q, g, :],
                                        ALU.mult).then_inc(masked_made, 1)

            def multiply(k, c, a, b):
                m = len(chunks[c])
                dve.wait_ge(factor_copied, k + 1)
                nc.vector.tensor_tensor(z[0:m, c, a:b], factor[0:m, k % 2, a:b], sel_banks(k)[1][0:m, a:b], ALU.mult).then_inc(z_made, 1)

            def split_big(r):
                a, b = (x // P for x in RANGES[r])
                s = sum_b[:, a:b, :]
                nc.vector.tensor_copy(parts_b[:, a:b, 0, :], s).then_inc(big_high, 1)
                dve.wait_ge(big_high, r + 1)
                nc.vector.tensor_tensor(rest_b[:, a:b, :], s, parts_b[:, a:b, 0, :], ALU.subtract).then_inc(big_rest, 1)
                dve.wait_ge(big_rest, r + 1)
                nc.vector.tensor_copy(parts_b[:, a:b, 1, :], rest_b[:, a:b, :]).then_inc(big_mid, 1)
                dve.wait_ge(big_mid, r + 1)
                nc.vector.tensor_tensor(parts_b[:, a:b, 2, :], rest_b[:, a:b, :], parts_b[:, a:b, 1, :],
                                        ALU.subtract).then_inc(big_parts, 1)

            make_masks(0)
            make_masks(1)
            for g in range(NG):
                sum_rows(g)
                split_sums(g)
                if g >= 1:
                    mask_picked(g - 1)
                if g + 2 < NG:
                    make_masks(g + 2)
                for s, c in enumerate(early[:-1]):
                    if g == snap_after[s] + 2:
                        multiply(s, c, 0, B)
            mask_picked(NG - 1)
            dve.wait_ge(big_summed, RANGES[0][1] // P)
            split_big(0)
            multiply(len(early) - 1, early[-1], 0, B)
            for k, c in enumerate(late):
                multiply(len(early) + k, c, *RANGES[0])
            t = TILES - 1
            dve.wait_ge(gathered[t], 16 * NBIG)
            nc.vector.tensor_reduce(sum_b[:, t, :], rows_b[:, t, :, :], AX.X, ALU.add).then_inc(big_summed, 1)
            dve.wait_ge(big_summed, TILES)
            split_big(1)
            for k, c in enumerate(late):
                multiply(len(early) + len(late) + k, c, *RANGES[1])

        @block.tensor
        def _(pe):
            def spread(g):
                f0, n, _ = groups[g]
                for h in range(2):
                    if n > 2 * h:
                        if g >= 1:
                            pe.wait_ge(row_copied, halves[g - 1] + h + 1)
                        for j in range(2 * h, min(2 * h + 2, n)):
                            i = nc.tensor.matmul(bank[h][:, j - 2 * h, :],
                                                 ident[0:NS, f0 + j:f0 + j + 1].broadcast_to([NS, P]),
                                                 row_b[:, :], start=True, stop=True)
                        i.then_inc(row_spread, 1)
                if g == 0:
                    pe.wait_ge(group_in, 16)
                if g >= 2:
                    pe.wait_ge(col_copied, g - 1)
                i = nc.tensor.matmul((SEL_A, SEL_B)[g % 2][0:n * QUAD, :],
                                     group_rows[:, g * P:g * P + n * QUAD],
                                     col_b[:, :], start=True, stop=True)
                i.then_inc(col_spread, 1)

            def pick(g):
                f0, n, _ = groups[g]
                pe.wait_ge(onehot_made, g + 1)
                pe.wait_ge(parts_made, g + 1)
                if g >= 1:
                    pe.wait_ge(masked_made, g)
                for j in range(n):
                    i = nc.tensor.matmul(PICK[j * QUAD:(j + 1) * QUAD, :], parts[:, f0 + j, :], onehot[:, f0 + j, :],
                                         start=True, stop=True)
                i.then_inc(picked, 1)

            def stack(g):
                q = groups[g][1] * QUAD
                if g == 0:
                    pe.wait_ge(select_in, 16)
                pe.wait_ge(masked_made, g + 1)
                done = sum(1 for s in snap_after if s < g)
                if done:
                    pe.wait_ge(snapped, done)
                nc.tensor.matmul(STACK[0:KS, :], gather_sum(g)[0:q, :], masked[0:q, g % 2, :],
                                 start=g == 0, stop=g == NG - 1, skip_group_check=True).then_inc(stacked, 1)

            def select_pairs(k, c, a, b):
                m = len(chunks[c])
                for side, bk in enumerate(sel_banks(k)):
                    mine = [kind for kind in "sb" if (c, side, kind) in uses]
                    for kind in mine:
                        src = (stack_s if kind == "s" else stack_b)[:, a:b]
                        i = nc.tensor.matmul(bk[0:m, a:b], selector(c, side, kind), src,
                                             start=kind == mine[0], stop=kind == mine[-1])
                i.then_inc(selected, 1)

            def layer1(c, a, b, n, last):
                k = len(chunks[c]) + (DENSE if c == NCH - 1 else 0)
                return nc.tensor.matmul(low[n][:, a:b], w1_s[0:k, c, n * P:(n + 1) * P], z[0:k, c, a:b],
                                        start=c == 0, stop=last, skip_group_check=True)

            def early_layer1(s):
                pe.wait_ge(z_made, s + 1)
                if s == 0:
                    pe.wait_ge(w1_in, 16)
                    pe.wait_ge(row_copied, halves[NG])
                for n in range(NB1):
                    layer1(early[s], 0, B, n, False)

            pe.wait_ge(ident_in, 16)
            pe.wait_ge(ids_cut_b, 2)
            ahead = 3
            for g in range(ahead):
                spread(g)
            for g in range(NG):
                if g >= 1:
                    stack(g - 1)
                if g - 1 in snap_after[:-1]:
                    pe.wait_ge(snapped, snap_after.index(g - 1) + 1)
                    pe.wait_ge(col_copied, NG)
                    s = snap_after.index(g - 1)
                    if s >= 1:
                        pe.wait_ge(z_made, s)
                    select_pairs(s, early[s], 0, B)
                pick(g)
                if g - 2 in snap_after[:-1]:
                    early_layer1(snap_after.index(g - 2))
                for x in (ahead + 2 * g, ahead + 2 * g + 1):
                    if x < NG:
                        spread(x)
            stack(NG - 1)
            s = len(early) - 1
            if NG - 2 in snap_after[:-1]:
                early_layer1(snap_after.index(NG - 2))
            pe.wait_ge(snapped, len(early))
            pe.wait_ge(z_made, s)
            select_pairs(s, early[s], 0, B)

            def turn_big(r):
                a, b = RANGES[r]
                to = STACK if r == 0 else SEL_B
                pe.wait_ge(big_parts, r + 1)
                for t in range(a // P, b // P):
                    i = nc.tensor.matmul(to[0:KB, t * P:(t + 1) * P], parts_b[:, t, :, :], ident[:, :],
                                         start=True, stop=True)
                i.then_inc(big_turned, 1)

            turn_big(0)
            early_layer1(s)
            pe.wait_ge(dense_in, 16)
            for r, (a, b) in enumerate(RANGES):
                base = len(early) + r * len(late)
                if r >= 1:
                    pe.wait_ge(y_made, r)
                    turn_big(r)
                pe.wait_ge(big_stacked, r + 1)
                for i in range(2):
                    select_pairs(base + i, late[i], a, b)
                pe.wait_ge(z_made, base + 1)
                select_pairs(base + 2, late[2], a, b)
                for i, c in enumerate(late):
                    pe.wait_ge(z_made, base + i + 1)
                    for n in range(NB1):
                        if r >= 1 and i == 0:
                            pe.wait_ge(h1_made, (r - 1) * NB1 + n + 1)
                        w = layer1(c, a, b, n, i == len(late) - 1)
                        if i == len(late) - 1:
                            w.then_inc(l1_done, 1)
                if r == 0:
                    pe.wait_ge(w2_in, 16)
                for m in range(NB2):
                    for n in range(NB1):
                        pe.wait_ge(h1_made, r * NB1 + n + 1)
                        w = nc.tensor.matmul((PICK, STACK)[m][:, a:b], w2_s[:, n, m * P:(m + 1) * P], h1[:, n, a:b],
                                             start=n == 0, stop=n == NB1 - 1)
                    w.then_inc(l2_done, 1)
                for m in range(NB2):
                    pe.wait_ge(h2_made, r * NB2 + m + 1)
                    w = nc.tensor.matmul(SEL_A[0:1, a:b], vec[:, V_W3 + m:V_W3 + m + 1], h2[:, m, a:b],
                                         start=m == 0, stop=m == NB2 - 1)
                w.then_inc(l3_done, 1)


def kernel(**inputs):
    import ml_dtypes
    import concourse.bacc as bacc
    from concourse.bass_utils import run_bass_kernel_spmd

    x = {k: np.asarray(v) for k, v in inputs.items()}
    tbl = [x[f"tbl_{f}"] for f in range(FIELDS)]
    rows = [t.shape[0] for t in tbl]
    small, big, cols, groups, chunks = plan(rows)
    NS, NBIG = len(small), len(big)
    KS, KB = PARTS * NS, PARTS * NBIG

    padded = []
    for f, c in zip(small, cols):
        t = np.concatenate([tbl[f], np.zeros((c * P - rows[f], D), tbl[f].dtype)])
        padded.append(t.reshape(c, P, D).transpose(1, 0, 2).reshape(P, c * D))
    tables = np.concatenate(padded, axis=1)
    ids = x["ids"]
    ids_small = np.ascontiguousarray(ids[:, small].T)
    idx_big = np.ascontiguousarray(ids[:, big].reshape(TILES, P, NBIG).transpose(1, 0, 2).reshape(P, TILES * NBIG))

    upper = {pair: k for k, pair in enumerate(zip(*np.triu_indices(FIELDS, k=1)))}
    field = {("s", i): f for i, f in enumerate(small)}
    field.update({("b", i): f for i, f in enumerate(big)})
    W = x["W_top1"]
    w1 = np.zeros((P, len(chunks), N1), W.dtype)
    for c, chunk in enumerate(chunks):
        at = [upper[tuple(sorted((field[a], field[b])))] for a, b in chunk]
        w1[:len(at), c] = W[at]
    w1[len(chunks[-1]):len(chunks[-1]) + DENSE, -1] = W[W.shape[0] - DENSE:]
    w2 = np.ascontiguousarray(x["W_top2"].reshape(NB1, P, N2).transpose(1, 0, 2))

    slot = np.arange(P) % QUAD
    column = np.where(slot < PARTS * CMAX, slot % CMAX, -1)
    vectors = np.concatenate([
        np.arange(P, dtype=np.float32)[:, None], column.astype(np.float32)[:, None],
        x["b_top1"].reshape(NB1, P).T, x["b_top2"].reshape(NB2, P).T, x["W_top3"].reshape(NB2, P).T], axis=1)
    ident = np.eye(P, dtype=ml_dtypes.bfloat16)
    group_rows = np.zeros((NS, len(groups) * P), ml_dtypes.bfloat16)
    for g, (f0, n, _) in enumerate(groups):
        for j in range(n):
            group_rows[f0 + j, g * P + j * QUAD:g * P + (j + 1) * QUAD] = 1
    uses = selectors(chunks, NS, NBIG)
    select = np.zeros((P, len(groups) * KS + len(uses) * P), ml_dtypes.bfloat16)
    for g, (f0, n, _) in enumerate(groups):
        for j in range(n):
            for q in range(PARTS * CMAX):
                select[j * QUAD + q, g * KS + q // CMAX * NS + f0 + j] = 1
    for u, (c, side, kind) in enumerate(uses):
        for m, pair in enumerate(chunks[c]):
            if pair[side][0] == kind:
                for k in range(PARTS):
                    select[k * (NS if kind == "s" else NBIG) + pair[side][1], len(groups) * KS + u * P + m] = 1

    nc = bacc.Bacc("TRN2", target_bir_lowering=False, num_devices=1)
    arrays = {
        "idx_big": idx_big, "ids_small": ids_small, "small_tables": tables,
        "dense": np.ascontiguousarray(x["dense_ctx"].T), "w1": w1, "w2": w2, "vectors": vectors,
        "ident": ident, "group_rows": group_rows, "select": select,
    }
    for f in big:
        arrays[f"big_table_{f}"] = tbl[f]
    ap = {n: nc.dram_tensor("in_" + n, a.shape, mybir.dt.from_np(a.dtype), kind="ExternalInput").ap() for n, a in arrays.items()}
    out = nc.dram_tensor("y_out", (B, 1), mybir.dt.float32, kind="ExternalOutput").ap()
    build(nc, rows, ap["idx_big"], ap["ids_small"], ap["small_tables"], [ap[f"big_table_{f}"] for f in big],
          ap["dense"], ap["w1"], ap["w2"], ap["vectors"], ap["ident"], ap["group_rows"], ap["select"], out)
    r = run_bass_kernel_spmd(nc, [{"in_" + n: a for n, a in arrays.items()}], core_ids=[0])
    return r.results[0]["y_out"]
```

```python
from contextlib import ExitStack

import numpy as np
import concourse.bass as bass
from concourse import mybir

P = 128
B = 512
D = 64
FIELDS = 39
DENSE = 16
PARTS = 3
SMALL_ROWS = 1280
CMAX = SMALL_ROWS // P
N1, N2 = 512, 256
NB1 = N1 // P
TILES = B // P
GROUP = 4
QUAD = 32
HALF = B // 2
assert PARTS * CMAX <= QUAD

RANGES = [(0, 256), (256, 384), (384, 512)]
FINISH = [(0, 256), (256, 512)]
SNAP_AFTER = [3, 5, 6, 7]
PICKS = [(0, 0, 256), (0, 256, 512), (1, 0, 256), (2, 0, 256), (2, 256, 512), (3, 0, 256), (1, 256, 384),
         (3, 256, 384), (4, 0, 256), (1, 384, 512), (3, 384, 512), (4, 256, 512), (5, 0, 256), (5, 256, 512)]
PIECES = [8, 8, 4, 4, 8, 8, 8, 4]
TURN_BEFORE = [5, 6, 8]


def plan(rows):
    small = sorted((f for f in range(FIELDS) if rows[f] <= SMALL_ROWS), key=lambda f: (-rows[f], f))
    big = [f for f in range(FIELDS) if rows[f] > SMALL_ROWS]
    cols = [-(-rows[f] // P) for f in small]
    groups = []
    at = 0
    while at < len(small):
        n = 1
        while n < GROUP and at + n < len(small) and cols[at + n] == cols[at]:
            n += 1
        groups.append((at, n, cols[at]))
        at += n
    ns, nb = len(small), len(big)
    known = []
    for i in range(ns):
        g = next(g for g, (f0, n, _) in enumerate(groups) if i < f0 + n)
        known.append(next(s for s, last in enumerate(SNAP_AFTER) if g <= last))
    ss = [(("s", i), ("s", j)) for j in range(ns) for i in range(j)]
    sb = [(("s", i), ("b", j)) for i in range(ns) for j in range(nb)]
    bb = [(("b", i), ("b", j)) for j in range(nb) for i in range(j)]

    def stage(pair):
        return max(known[x[1]] for x in pair if x[0] == "s")

    def of(pairs, s):
        return [p for p in pairs if stage(p) == s]

    first, second = of(ss, 0), of(ss, 1)
    assert len(first) <= P <= len(second)
    rest = bb + of(sb, 0) + second[P:] + of(sb, 1)
    for s in range(2, len(SNAP_AFTER)):
        rest += of(ss, s) + of(sb, s)
    chunks = [first, rest[:P], second[:P]] + [rest[i:i + P] for i in range(P, len(rest), P)]
    assert len(chunks[-1]) + DENSE <= P
    needs = [max(stage(p) for p in chunk if p[0][0] == "s") for chunk in chunks]
    return small, big, cols, groups, chunks, needs


def selectors(chunks, ns, nb):
    use = []
    for c, chunk in enumerate(chunks):
        for side in (0, 1):
            for kind in "sb":
                if any(pair[side][0] == kind for pair in chunk):
                    use.append((c, side, kind))
    return use


def build(nc, rows, idx_big, ids_small, tables, big_tables, dense, w1, w2, vectors, tail_rows, ident_c, group_c, add_c,
          select_c, out):
    f32, bf16, i32 = mybir.dt.float32, mybir.dt.bfloat16, mybir.dt.int32
    ALU = mybir.AluOpType
    ACT = mybir.ActivationFunctionType
    AX = mybir.AxisListType

    small, big, cols, groups, chunks, needs = plan(rows)
    NS, NBIG, NG, NCH = len(small), len(big), len(groups), len(chunks)
    KS, KB = PARTS * NS, PARTS * NBIG
    col0 = [sum(cols[:f]) for f in range(NS + 1)]
    uses = selectors(chunks, NS, NBIG)
    with_big = [any(b[0] == "b" for _, b in chunk) for chunk in chunks]
    assert all(b - a <= HALF for _, a, b in PICKS)
    assert SNAP_AFTER[-1] == NG - 1 and TURN_BEFORE[-1] == NG and PICKS[-1][0] == NCH - 1
    NP5 = len(chunks[-1])
    V_P, V_C, V_B1 = 0, 1, 2

    with ExitStack() as ctx:
        def sb(name, shape, dt):
            return ctx.enter_context(nc.sbuf_tensor(name, shape, dt))

        def sem(name):
            return ctx.enter_context(nc.semaphore(name))

        table = sb("table", [P, col0[NS] * D], f32)
        row_sum = sb("row_sum", [P, col0[NS]], f32)
        rest = sb("rest", [P, 2, GROUP * CMAX], f32)
        parts = sb("parts", [P, NS, QUAD], bf16)
        ids_s = sb("ids_s", [P, B], i32)
        row_i = sb("row_i", [P, B], i32)
        col_i = sb("col_i", [P, B], i32)
        row_b = sb("row_b", [P, B], bf16)
        col_b = sb("col_b", [P, B], bf16)
        onehot = sb("onehot", [P, NS, B], bf16)
        col_mask = sb("col_mask", [P, NG, B], bf16)
        masked = sb("masked", [P, 2, B], bf16)
        stack_s = sb("stack_s", [KS, len(SNAP_AFTER), B], bf16)
        idx = sb("idx", [P, TILES * NBIG], i32)
        rows_b = sb("rows_b", [P, TILES, NBIG, D], f32)
        sum_b = sb("sum_b", [P, TILES, NBIG], f32)
        rest_b = sb("rest_b", [P, TILES, NBIG], f32)
        parts_b = sb("parts_b", [P, TILES, PARTS, NBIG], bf16)
        stack_b = sb("stack_b", [KB, B], bf16)
        factor = sb("factor", [P, 2, B], f32)
        z = sb("z", [P, NCH, B], f32)
        w1_s = sb("w1_s", [P, NCH, N1], f32)
        w2_s = sb("w2_s", [P, NB1, N2], f32)
        vec = sb("vec", [P, V_B1 + NB1], f32)
        tail = sb("tail", [P, 2, N2], f32)
        ident = sb("ident", [P, P], bf16)
        group_rows = sb("group_rows", [NS, NG * P], bf16)
        add_cols = sb("add_cols", [P, NG * KS], bf16)
        select = sb("select", [KS, len(uses) * P], bf16)
        h1 = sb("h1", [P, NB1, B], f32)
        h2 = sb("h2", [P, TILES, N2], f32)
        h2_w3 = sb("h2_w3", [P, TILES, N2], f32)
        y = sb("y", [P, TILES], f32)

        bank = [ctx.enter_context(nc.psum_tensor(f"bank{i}", [P, 2, B], f32)) for i in range(2)]
        low = [bank[0][:, 0, :], bank[0][:, 1, :], bank[1][:, 0, :], bank[1][:, 1, :]]
        high = [ctx.enter_context(nc.psum_tensor(f"bank{i}", [P, B], f32)) for i in range(4, 8)]
        PICK, STACK = high[0], high[2]
        SEL_A, SEL_B = high[1], high[3]
        SEL = (SEL_A, SEL_B)
        L2_BANKS = (PICK, STACK, SEL_A, SEL_B)
        sel_b = [x[:, :].rearrange("p (s c n) -> p s c n", s=2, c=2) for x in (SEL_A, SEL_B)]

        def adder(g):
            return add_cols[:, g * KS:(g + 1) * KS]

        def selector(c, side, kind, m):
            u = uses.index((c, side, kind))
            return select[0:KS if kind == "s" else KB, u * P:u * P + m]

        ids_in, idx_in, ident_in, vec_in, group_in = (
            sem("ids_in"), sem("idx_in"), sem("ident_in"), sem("vec_in"), sem("group_in"))
        add_in, select_in, dense_in, w2_in = sem("add_in"), sem("select_in"), sem("dense_in"), sem("w2_in")
        w1_in = [sem(f"w1_in{c}") for c in range(NCH)]
        table_in = [sem(f"table_in{g}") for g in range(NG)]
        gathered = [sem(f"gathered{t}") for t in range(TILES)]
        out_written = sem("out_written")
        parts_zeroed = sem("parts_zeroed")
        ids_cut, ids_cut_b = sem("ids_cut"), sem("ids_cut_b")
        row_spread, row_copied = sem("row_spread"), sem("row_copied")
        col_spread, col_copied = sem("col_spread"), sem("col_copied")
        onehot_made, mask_made = sem("onehot_made"), sem("mask_made")
        rows_summed, high_made, rest_made, mid_made, parts_made = (
            sem("rows_summed"), sem("high_made"), sem("rest_made"), sem("mid_made"), sem("parts_made"))
        picked, masked_made, stacked, snapped = sem("picked"), sem("masked_made"), sem("stacked"), sem("snapped")
        big_summed, big_high, big_rest, big_mid, big_parts = (
            sem("big_summed"), sem("big_high"), sem("big_rest"), sem("big_mid"), sem("big_parts"))
        big_turned, big_stacked = sem("big_turned"), sem("big_stacked")
        selected, factor_copied, z_made = sem("selected"), sem("factor_copied"), sem("z_made")
        l1_done, h1_made, l2_done, h2_made, y_made = (
            sem("l1_done"), sem("h1_made"), sem("l2_done"), sem("h2_made"), sem("y_made"))
        tail_in = sem("tail_in")

        block = ctx.enter_context(nc.Block())

        def halves(g):
            return sum(-(-n // 2) for _, n, _ in groups[:g])

        def factors(k):
            _, a, b = PICKS[k]
            return SEL[k % 2][:, 0:b - a], SEL[k % 2][:, HALF:HALF + b - a]

        @block.sync
        def _(sp):
            def load_table(g):
                f0, n, c = groups[g]
                pieces = PIECES[g]
                for h in range(pieces):
                    a, b = (col0[f0] + h * n * c // pieces) * D, (col0[f0] + (h + 1) * n * c // pieces) * D
                    sp.dma_start(table[:, a:b], tables[:, a:b]).then_inc(table_in[g], 16)

            def load_w1(c):
                sp.dma_start(w1_s[:, c, :], w1[:, c, :]).then_inc(w1_in[c], 16)

            sp.dma_start(ids_s[:, :], ids_small).then_inc(ids_in, 16)
            sp.dma_start(vec[:, :], vectors).then_inc(vec_in, 16)
            load_table(0)
            sp.dma_start(add_cols[:, :], add_c).then_inc(add_in, 16)
            for g in range(1, NG):
                load_table(g)
                if g == 3:
                    sp.dma_start(select[:, :], select_c).then_inc(select_in, 16)
                if g == 4:
                    load_w1(0)
                if g == 5:
                    load_w1(1)
            for c in range(2, NCH):
                load_w1(c)
            sp.dma_start(z[NP5:NP5 + DENSE, NCH - 1, :], dense).then_inc(dense_in, 16)
            sp.dma_start(w2_s[:, :, :], w2).then_inc(w2_in, 16)
            sp.dma_start(tail[:, :, :], tail_rows.broadcast_to([P, 2, N2])).then_inc(tail_in, 16)
            sp.wait_ge(y_made, TILES)
            sp.dma_start(out.rearrange("(p t) one -> p (t one)", t=TILES), y[:, :]).then_inc(out_written, 16)
            sp.wait_ge(out_written, 16)

        @block.gpsimd
        def _(pool):
            pool.wait_ge(idx_in, 16)
            for t in range(TILES):
                for f in range(NBIG):
                    k = t * NBIG + f
                    nc.gpsimd.indirect_dma_start(
                        rows_b[:, t, f, :], None, big_tables[f],
                        bass.IndirectOffsetOnAxis(ap=idx[:, k:k + 1], axis=0)).then_inc(gathered[t], 16)

        @block.scalar
        def _(act):
            act.dma_start(idx[:, :], idx_big).then_inc(idx_in, 16)
            act.dma_start(ident[:, :], ident_c).then_inc(ident_in, 16)
            act.dma_start(group_rows[:, :], group_c).then_inc(group_in, 16)

            def copy_rows(g, h):
                f0, n, _ = groups[g]
                m = min(2, n - 2 * h)
                act.wait_ge(row_spread, halves(g) + h + 1)
                nc.scalar.copy(onehot[:, f0 + 2 * h:f0 + 2 * h + m, :], bank[h][:, 0:m, :]).then_inc(row_copied, 1)

            def copy_cols(g):
                q = groups[g][1] * QUAD
                act.wait_ge(col_spread, g + 1)
                nc.scalar.copy(col_mask[0:q, g, :], SEL_B[0:q, :]).then_inc(col_copied, 1)

            def snap(s):
                act.wait_ge(stacked, SNAP_AFTER[s] + 1)
                nc.scalar.copy(stack_s[:, s, :], STACK[0:KS, :]).then_inc(snapped, 1)

            def copy_factor(k):
                c, a, b = PICKS[k]
                m = len(chunks[c])
                act.wait_ge(selected, k + 1)
                if k >= 2:
                    act.wait_ge(z_made, k - 1)
                nc.scalar.copy(factor[0:m, k % 2, 0:b - a], factors(k)[0][0:m]).then_inc(factor_copied, 1)

            def sum_big(t, h):
                if h == 0:
                    act.wait_ge(gathered[t], 16 * NBIG)
                for f in range(h * NBIG // 2, (h + 1) * NBIG // 2):
                    i = nc.scalar.activation(rows_b[:, t, f, :], rows_b[:, t, f, :], ACT.Copy,
                                             accum_out=sum_b[:, t, f:f + 1])
                if h == 1:
                    i.then_inc(big_summed, 1)

            def copy_turned(r):
                a, b = RANGES[r]
                act.wait_ge(big_turned, r + 1)
                nc.scalar.copy(stack_b[:, a:b], PICK[0:KB, a:b]).then_inc(big_stacked, 1)

            def relu1(r, n):
                a, b = FINISH[r]
                if r == 0 and n == 0:
                    act.wait_ge(vec_in, 16)
                act.wait_ge(l1_done, r * NB1 + n + 1)
                nc.scalar.activation(h1[:, n, a:b], low[n][:, a:b], ACT.Relu,
                                     bias=vec[:, V_B1 + n:V_B1 + n + 1]).then_inc(h1_made, 1)

            copy_rows(0, 0)
            copy_rows(0, 1)
            copy_cols(0)
            copy_rows(1, 0)
            copy_rows(1, 1)
            copy_cols(1)
            copy_rows(2, 0)
            copy_cols(2)
            copy_rows(2, 1)
            copy_rows(3, 0)
            copy_cols(3)
            copy_rows(3, 1)
            copy_cols(4)
            copy_rows(4, 0)
            copy_cols(5)
            copy_rows(4, 1)
            copy_rows(5, 0)
            copy_cols(6)
            copy_rows(5, 1)
            copy_cols(7)
            sum_big(0, 0)
            sum_big(0, 1)
            copy_rows(6, 0)
            copy_rows(6, 1)
            copy_rows(7, 0)
            snap(0)
            copy_factor(0)
            copy_factor(1)
            sum_big(1, 0)
            sum_big(1, 1)
            copy_turned(0)
            copy_factor(2)
            snap(1)
            copy_factor(3)
            copy_factor(4)
            sum_big(2, 0)
            sum_big(2, 1)
            copy_factor(5)
            copy_turned(1)
            copy_factor(6)
            snap(2)
            copy_factor(7)
            copy_factor(8)
            copy_turned(2)
            snap(3)
            for n in range(9, 14):
                copy_factor(n)
            for n in range(4):
                relu1(0, n)
            for n in range(4):
                relu1(1, n)

        @block.vector
        def _(dve):
            nc.vector.memset(parts[:, :, :], 0.0).then_inc(parts_zeroed, 1)
            dve.wait_ge(ids_in, 16)
            nc.vector.tensor_single_scalar(row_i[:, :], ids_s[:, :], P - 1, ALU.bitwise_and).then_inc(ids_cut, 1)
            dve.wait_ge(ids_cut, 1)
            nc.vector.tensor_copy(row_b[:, :], row_i[:, :]).then_inc(ids_cut_b, 1)
            nc.vector.tensor_single_scalar(col_i[:, :], ids_s[:, :], 7, ALU.logical_shift_right).then_inc(ids_cut, 1)
            dve.wait_ge(ids_cut, 2)
            nc.vector.tensor_copy(col_b[:, :], col_i[:, :]).then_inc(ids_cut_b, 1)
            dve.wait_ge(vec_in, 16)

            def make_onehot(g):
                f0, n, _ = groups[g]
                dve.wait_ge(row_copied, halves(g + 1))
                nc.vector.tensor_scalar(onehot[:, f0:f0 + n, :], onehot[:, f0:f0 + n, :], vec[:, V_P:V_P + 1],
                                        None, ALU.is_equal).then_inc(onehot_made, 1)

            def make_mask(g):
                q = groups[g][1] * QUAD
                dve.wait_ge(col_copied, g + 1)
                nc.vector.tensor_scalar(col_mask[0:q, g, :], col_mask[0:q, g, :], vec[0:q, V_C:V_C + 1],
                                        None, ALU.is_equal).then_inc(mask_made, 1)

            def sum_rows(g):
                f0, n, c = groups[g]
                a, b = col0[f0], col0[f0 + n]
                dve.wait_ge(table_in[g], 16 * PIECES[g])
                src = table[:, a * D:b * D].rearrange("p (r d) -> p r d", d=D)
                nc.vector.tensor_reduce(row_sum[:, a:b], src, AX.X, ALU.add).then_inc(rows_summed, 1)

            def split_sums(g, step):
                f0, n, c = groups[g]
                s = row_sum[:, col0[f0]:col0[f0 + n]].rearrange("p (f c) -> p f c", c=c)
                part = [parts[:, f0:f0 + n, k * CMAX:k * CMAX + c] for k in range(PARTS)]
                r = rest[:, g % 2, 0:n * c].rearrange("p (f c) -> p f c", c=c)
                if step == 0:
                    dve.wait_ge(rows_summed, g + 1)
                    if g == 0:
                        dve.wait_ge(parts_zeroed, 1)
                    nc.vector.tensor_copy(part[0], s).then_inc(high_made, 1)
                elif step == 1:
                    dve.wait_ge(high_made, g + 1)
                    nc.vector.tensor_tensor(r, s, part[0], ALU.subtract).then_inc(rest_made, 1)
                elif step == 2:
                    dve.wait_ge(rest_made, g + 1)
                    nc.vector.tensor_copy(part[1], r).then_inc(mid_made, 1)
                else:
                    dve.wait_ge(mid_made, g + 1)
                    nc.vector.tensor_tensor(part[2], r, part[1], ALU.subtract).then_inc(parts_made, 1)

            def mask_picked(g):
                q = groups[g][1] * QUAD
                dve.wait_ge(mask_made, g + 1)
                dve.wait_ge(picked, g + 1)
                if g >= 2:
                    dve.wait_ge(stacked, g - 1)
                nc.vector.tensor_tensor(masked[0:q, g % 2, :], PICK[0:q, :], col_mask[0:q, g, :],
                                        ALU.mult).then_inc(masked_made, 1)

            def multiply(k):
                c, a, b = PICKS[k]
                m = len(chunks[c])
                dve.wait_ge(factor_copied, k + 1)
                nc.vector.tensor_tensor(z[0:m, c, a:b], factor[0:m, k % 2, 0:b - a], factors(k)[1][0:m],
                                        ALU.mult).then_inc(z_made, 1)

            def sum_big(t):
                dve.wait_ge(gathered[t], 16 * NBIG)
                nc.vector.tensor_reduce(sum_b[:, t, :], rows_b[:, t, :, :], AX.X, ALU.add).then_inc(big_summed, 1)

            def split_big(r, step):
                a, b = (x // P for x in RANGES[r])
                s, high, mid = sum_b[:, a:b, :], parts_b[:, a:b, 0, :], parts_b[:, a:b, 1, :]
                rest = rest_b[:, a:b, :]
                if step == 0:
                    dve.wait_ge(big_summed, b)
                    nc.vector.tensor_copy(high, s).then_inc(big_high, 1)
                elif step == 1:
                    dve.wait_ge(big_high, r + 1)
                    nc.vector.tensor_tensor(rest, s, high, ALU.subtract).then_inc(big_rest, 1)
                elif step == 2:
                    dve.wait_ge(big_rest, r + 1)
                    nc.vector.tensor_copy(mid, rest).then_inc(big_mid, 1)
                else:
                    dve.wait_ge(big_mid, r + 1)
                    nc.vector.tensor_tensor(parts_b[:, a:b, 2, :], rest, mid, ALU.subtract).then_inc(big_parts, 1)

            def finish(t):
                if t == 0:
                    dve.wait_ge(tail_in, 16)
                dve.wait_ge(l2_done, t + 1)
                nc.vector.tensor_tensor(h2[:, t, :], L2_BANKS[t][:, 0:N2], tail[:, 0, :], ALU.add).then_inc(h2_made, 1)
                dve.wait_ge(h2_made, t + 1)
                nc.vector.scalar_tensor_tensor(h2_w3[:, t, :], h2[:, t, :], 0.0, tail[:, 1, :], ALU.max, ALU.mult,
                                               accum_out=y[:, t:t + 1]).then_inc(y_made, 1)

            make_onehot(0)
            make_mask(0)
            sum_rows(0)
            make_mask(1)
            split_sums(0, 0)
            make_mask(2)
            split_sums(0, 1)
            make_onehot(1)
            split_sums(0, 2)
            split_sums(0, 3)
            make_onehot(2)
            sum_rows(1)
            mask_picked(0)
            split_sums(1, 0)
            make_mask(3)
            split_sums(1, 1)
            sum_rows(2)
            split_sums(1, 2)
            make_mask(4)
            split_sums(1, 3)
            make_mask(5)
            split_sums(2, 0)
            make_mask(6)
            mask_picked(1)
            split_sums(2, 1)
            sum_rows(3)
            split_sums(2, 2)
            make_mask(7)
            split_sums(2, 3)
            split_sums(3, 0)
            split_sums(3, 1)
            make_onehot(3)
            mask_picked(2)
            split_sums(3, 2)
            split_sums(3, 3)
            make_onehot(4)
            make_onehot(5)
            mask_picked(3)
            sum_rows(4)
            split_sums(4, 0)
            split_sums(4, 1)
            multiply(0)
            split_sums(4, 2)
            multiply(1)
            split_sums(4, 3)
            sum_rows(5)
            split_big(0, 0)
            split_sums(5, 0)
            split_big(0, 1)
            split_sums(5, 1)
            split_big(0, 2)
            split_sums(5, 2)
            split_big(0, 3)
            split_sums(5, 3)
            mask_picked(4)
            sum_rows(6)
            mask_picked(5)
            split_sums(6, 0)
            multiply(2)
            split_sums(6, 1)
            sum_rows(7)
            split_sums(6, 2)
            split_sums(6, 3)
            multiply(3)
            split_sums(7, 0)
            multiply(4)
            make_onehot(6)
            split_sums(7, 1)
            make_onehot(7)
            split_sums(7, 2)
            split_sums(7, 3)
            split_big(1, 0)
            split_big(1, 1)
            multiply(5)
            split_big(1, 2)
            split_big(1, 3)
            sum_big(3)
            mask_picked(6)
            multiply(6)
            for n in range(4):
                split_big(2, n)
            mask_picked(7)
            for n in range(7, 14):
                multiply(n)
            for n in range(4):
                finish(n)

        @block.tensor
        def _(pe):
            def spread_rows(g, h):
                f0, n, _ = groups[g]
                if g >= 1:
                    pe.wait_ge(row_copied, halves(g - 1) + min(h + 1, halves(g) - halves(g - 1)))
                for j in range(2 * h, min(2 * h + 2, n)):
                    i = nc.tensor.matmul(low[j], ident[:, f0 + j:f0 + j + 1].broadcast_to([P, P]), row_b[:, :],
                                         start=True, stop=True)
                i.then_inc(row_spread, 1)

            def spread_cols(g):
                q = groups[g][1] * QUAD
                if g == 0:
                    pe.wait_ge(group_in, 16)
                    pe.wait_ge(ids_cut_b, 2)
                else:
                    pe.wait_ge(col_copied, g)
                nc.tensor.matmul(SEL_B[0:q, :], group_rows[:, g * P:g * P + q],
                                 col_b[0:NS, :], start=True, stop=True).then_inc(col_spread, 1)

            def pick(g):
                f0, n, _ = groups[g]
                pe.wait_ge(onehot_made, g + 1)
                pe.wait_ge(parts_made, g + 1)
                if g >= 1:
                    pe.wait_ge(masked_made, g)
                if g in TURN_BEFORE:
                    pe.wait_ge(big_stacked, TURN_BEFORE.index(g) + 1)
                for j in range(n):
                    i = nc.tensor.matmul(PICK[j * QUAD:(j + 1) * QUAD, :], parts[:, f0 + j, :], onehot[:, f0 + j, :],
                                         start=True, stop=True)
                i.then_inc(picked, 1)

            def stack(g):
                q = groups[g][1] * QUAD
                if g == 0:
                    pe.wait_ge(add_in, 16)
                pe.wait_ge(masked_made, g + 1)
                done = sum(1 for last in SNAP_AFTER if last < g)
                if done:
                    pe.wait_ge(snapped, done)
                nc.tensor.matmul(STACK[0:KS, :], adder(g)[0:q, :], masked[0:q, g % 2, :],
                                 start=g == 0, stop=g == NG - 1, skip_group_check=True).then_inc(stacked, 1)

            def select_pairs(k):
                c, a, b = PICKS[k]
                m, s = len(chunks[c]), needs[c]
                pe.wait_ge(snapped, s + 1)
                if with_big[c]:
                    pe.wait_ge(big_stacked, sum(1 for _, end in RANGES if end <= b))
                if k == 0:
                    pe.wait_ge(select_in, 16)
                elif k == 1:
                    pe.wait_ge(col_copied, NG)
                else:
                    pe.wait_ge(z_made, k - 1)
                for side, to in enumerate(factors(k)):
                    mine = [kind for kind in "sb" if (c, side, kind) in uses]
                    for kind in mine:
                        src = stack_s[:, s, a:b] if kind == "s" else stack_b[:, a:b]
                        i = nc.tensor.matmul(to[0:m], selector(c, side, kind, m), src,
                                             start=kind == mine[0], stop=kind == mine[-1])
                i.then_inc(selected, 1)

            def turn_big(r):
                a, b = RANGES[r]
                pe.wait_ge(big_parts, r + 1)
                pe.wait_ge(masked_made, TURN_BEFORE[r])
                for t in range(a // P, b // P):
                    i = nc.tensor.matmul(PICK[0:KB, t * P:(t + 1) * P], parts_b[:, t, :, :], ident[:, :],
                                         start=True, stop=True)
                i.then_inc(big_turned, 1)

            def layer1(k, h):
                c, a, b = PICKS[k]
                if k == 0:
                    pe.wait_ge(row_copied, halves(NG))
                if c == NCH - 1:
                    pe.wait_ge(dense_in, 16)
                pe.wait_ge(w1_in[c], 16)
                pe.wait_ge(z_made, k + 1)
                rows_c = len(chunks[c]) + (DENSE if c == NCH - 1 else 0)
                done = sum(1 for _, end in FINISH if end <= a)
                for n in (2 * h, 2 * h + 1):
                    if done and c == NCH - 1:
                        pe.wait_ge(h1_made, (done - 1) * NB1 + n + 1)
                    w = nc.tensor.matmul(low[n][:, a:b], w1_s[0:rows_c, c, n * P:(n + 1) * P], z[0:rows_c, c, a:b],
                                         start=k == 0, stop=c == NCH - 1, skip_group_check=True)
                    if c == NCH - 1 and b in [end for _, end in FINISH]:
                        w.then_inc(l1_done, 1)

            def layer2(t):
                if t == 0:
                    pe.wait_ge(w2_in, 16)
                    pe.wait_ge(big_stacked, len(RANGES))
                if t == 1:
                    pe.wait_ge(snapped, len(SNAP_AFTER))
                if t == 2:
                    pe.wait_ge(z_made, len(PICKS))
                r = next(r for r, (_, end) in enumerate(FINISH) if t * P < end)
                for n in range(NB1):
                    pe.wait_ge(h1_made, r * NB1 + n + 1)
                    w = nc.tensor.matmul(L2_BANKS[t][:, 0:N2], h1[:, n, t * P:(t + 1) * P], w2_s[:, n, :],
                                         start=n == 0, stop=n == NB1 - 1)
                w.then_inc(l2_done, 1)

            pe.wait_ge(ident_in, 16)
            pe.wait_ge(ids_cut_b, 1)
            spread_rows(0, 0)
            spread_rows(0, 1)
            spread_cols(0)
            spread_rows(1, 0)
            spread_rows(1, 1)
            spread_cols(1)
            spread_rows(2, 0)
            spread_rows(2, 1)
            spread_cols(2)
            spread_rows(3, 0)
            spread_cols(3)
            spread_rows(3, 1)
            pick(0)
            spread_cols(4)
            spread_rows(4, 0)
            spread_rows(4, 1)
            spread_cols(5)
            spread_rows(5, 0)
            spread_cols(6)
            stack(0)
            spread_rows(5, 1)
            spread_rows(6, 0)
            spread_cols(7)
            spread_rows(6, 1)
            pick(1)
            stack(1)
            spread_rows(7, 0)
            pick(2)
            stack(2)
            pick(3)
            stack(3)
            select_pairs(0)
            select_pairs(1)
            layer1(0, 0)
            pick(4)
            layer1(0, 1)
            stack(4)
            turn_big(0)
            layer1(1, 0)
            pick(5)
            select_pairs(2)
            layer1(1, 1)
            stack(5)
            layer1(2, 0)
            select_pairs(3)
            select_pairs(4)
            layer1(2, 1)
            layer1(3, 0)
            select_pairs(5)
            layer1(3, 1)
            layer1(4, 0)
            layer1(4, 1)
            turn_big(1)
            layer1(5, 0)
            pick(6)
            select_pairs(6)
            layer1(5, 1)
            stack(6)
            select_pairs(7)
            pick(7)
            layer1(6, 0)
            select_pairs(8)
            layer1(6, 1)
            layer1(7, 0)
            layer1(7, 1)
            stack(7)
            turn_big(2)
            layer1(8, 0)
            select_pairs(9)
            select_pairs(10)
            layer1(8, 1)
            layer1(9, 0)
            layer1(9, 1)
            select_pairs(11)
            select_pairs(12)
            layer1(10, 0)
            layer1(10, 1)
            layer1(11, 0)
            select_pairs(13)
            layer1(11, 1)
            layer1(12, 0)
            layer1(12, 1)
            layer1(13, 0)
            layer1(13, 1)
            for n in range(4):
                layer2(n)


def kernel(**inputs):
    import ml_dtypes
    import concourse.bacc as bacc
    from concourse.bass_utils import run_bass_kernel_spmd

    x = {k: np.asarray(v) for k, v in inputs.items()}
    tbl = [x[f"tbl_{f}"] for f in range(FIELDS)]
    rows = [t.shape[0] for t in tbl]
    small, big, cols, groups, chunks, _ = plan(rows)
    NS, NBIG = len(small), len(big)
    KS, KB = PARTS * NS, PARTS * NBIG

    padded = []
    for f, c in zip(small, cols):
        t = np.concatenate([tbl[f], np.zeros((c * P - rows[f], D), tbl[f].dtype)])
        padded.append(t.reshape(c, P, D).transpose(1, 0, 2).reshape(P, c * D))
    tables = np.concatenate(padded, axis=1)
    order = np.arange(B).reshape(P, TILES).T.reshape(B)
    ids = x["ids"][order]
    ids_small = np.zeros((P // QUAD, QUAD, B), ids.dtype)
    ids_small[:, :NS] = ids[:, small].T
    ids_small = ids_small.reshape(P, B)
    idx_big = np.ascontiguousarray(ids[:, big].reshape(TILES, P, NBIG).transpose(1, 0, 2).reshape(P, TILES * NBIG))

    upper = {pair: k for k, pair in enumerate(zip(*np.triu_indices(FIELDS, k=1)))}
    field = {("s", i): f for i, f in enumerate(small)}
    field.update({("b", i): f for i, f in enumerate(big)})
    W = x["W_top1"]
    w1 = np.zeros((P, len(chunks), N1), W.dtype)
    for c, chunk in enumerate(chunks):
        at = [upper[tuple(sorted((field[a], field[b])))] for a, b in chunk]
        w1[:len(at), c] = W[at]
    w1[len(chunks[-1]):len(chunks[-1]) + DENSE, -1] = W[W.shape[0] - DENSE:]
    w2 = np.ascontiguousarray(x["W_top2"].reshape(NB1, P, N2).transpose(1, 0, 2))

    slot = np.arange(P) % QUAD
    column = np.where(slot < PARTS * CMAX, slot % CMAX, -1)
    vectors = np.concatenate([
        np.arange(P, dtype=np.float32)[:, None], column.astype(np.float32)[:, None],
        x["b_top1"].reshape(NB1, P).T], axis=1)
    tail_rows = np.stack([x["b_top2"].reshape(N2), x["W_top3"].reshape(N2)])[None]
    ident = np.eye(P, dtype=ml_dtypes.bfloat16)
    group_rows = np.zeros((NS, len(groups) * P), ml_dtypes.bfloat16)
    for g, (f0, n, _) in enumerate(groups):
        for j in range(n):
            group_rows[f0 + j, g * P + j * QUAD:g * P + (j + 1) * QUAD] = 1
    uses = selectors(chunks, NS, NBIG)
    add_cols = np.zeros((P, len(groups) * KS), ml_dtypes.bfloat16)
    for g, (f0, n, _) in enumerate(groups):
        for j in range(n):
            for q in range(PARTS * CMAX):
                add_cols[j * QUAD + q, g * KS + q // CMAX * NS + f0 + j] = 1
    select = np.zeros((KS, len(uses) * P), ml_dtypes.bfloat16)
    for u, (c, side, kind) in enumerate(uses):
        for m, pair in enumerate(chunks[c]):
            if pair[side][0] == kind:
                for k in range(PARTS):
                    select[k * (NS if kind == "s" else NBIG) + pair[side][1], u * P + m] = 1

    nc = bacc.Bacc("TRN2", target_bir_lowering=False, num_devices=1)
    arrays = {
        "idx_big": idx_big, "ids_small": ids_small, "small_tables": tables,
        "dense": np.ascontiguousarray(x["dense_ctx"][order].T), "w1": w1, "w2": w2, "vectors": vectors, "tail_rows": tail_rows,
        "ident": ident, "group_rows": group_rows, "add_cols": add_cols, "select": select,
    }
    for f in big:
        arrays[f"big_table_{f}"] = tbl[f]
    ap = {n: nc.dram_tensor("in_" + n, a.shape, mybir.dt.from_np(a.dtype), kind="ExternalInput").ap() for n, a in arrays.items()}
    out = nc.dram_tensor("y_out", (B, 1), mybir.dt.float32, kind="ExternalOutput").ap()
    build(nc, rows, ap["idx_big"], ap["ids_small"], ap["small_tables"], [ap[f"big_table_{f}"] for f in big],
          ap["dense"], ap["w1"], ap["w2"], ap["vectors"], ap["tail_rows"], ap["ident"], ap["group_rows"], ap["add_cols"], ap["select"], out)
    r = run_bass_kernel_spmd(nc, [{"in_" + n: a for n, a in arrays.items()}], core_ids=[0])
    return r.results[0]["y_out"]
```

```python
from contextlib import ExitStack

import numpy as np
import concourse.bass as bass
from concourse import mybir

P = 128
B = 512
D = 64
FIELDS = 39
DENSE = 16
PARTS = 3
SMALL_ROWS = 1280
CMAX = SMALL_ROWS // P
N1, N2 = 512, 256
NB1 = N1 // P
TILES = B // P
GROUP = 4
QUAD = 32
HALF = B // 2
assert PARTS * CMAX <= QUAD

RANGES = [(0, 256), (256, 384), (384, 512)]
FINISH = [(0, 256), (256, 512)]
SNAP_AFTER = [3, 5, 6, 7]
PICKS = [(0, 0, 256), (0, 256, 512), (1, 0, 256), (2, 256, 512), (3, 0, 256), (2, 0, 256), (4, 0, 256),
         (3, 256, 384), (1, 256, 384), (3, 384, 512), (1, 384, 512), (5, 0, 256), (4, 256, 512), (5, 256, 512)]
PIECES = [2, 2, 1, 2, 2, 2, 2, 2]

def plan(rows):
    big = [f for f in range(FIELDS) if rows[f] > SMALL_ROWS]
    batches = []
    for c in range(1, CMAX + 1):
        fields = [f for f in range(FIELDS) if -(-rows[f] // P) == c]
        batches += [(fields[i:i + GROUP], c) for i in range(0, len(fields), GROUP)]
    batches.sort(key=lambda b: (len(b[0]) < GROUP, b[1] if len(b[0]) == GROUP else -b[1] * len(b[0])))
    small, cols, groups = [], [], []
    for fields, c in batches:
        groups.append((len(small), len(fields), c))
        small += fields
        cols += [c] * len(fields)
    ns, nb = len(small), len(big)
    known = []
    for i in range(ns):
        g = next(g for g, (f0, n, _) in enumerate(groups) if i < f0 + n)
        known.append(next(s for s, last in enumerate(SNAP_AFTER) if g <= last))
    ss = [(("s", i), ("s", j)) for j in range(ns) for i in range(j)]
    sb = [(("s", i), ("b", j)) for i in range(ns) for j in range(nb)]
    bb = [(("b", i), ("b", j)) for j in range(nb) for i in range(j)]

    def stage(pair):
        return max(known[x[1]] for x in pair if x[0] == "s")

    def of(pairs, s):
        return [p for p in pairs if stage(p) == s]

    first, second = of(ss, 0), of(ss, 1)
    assert len(first) <= P <= len(second)
    rest = bb + of(sb, 0) + second[P:] + of(sb, 1)
    for s in range(2, len(SNAP_AFTER)):
        rest += of(ss, s) + of(sb, s)
    chunks = [first, rest[:P], second[:P]] + [rest[i:i + P] for i in range(P, len(rest), P)]
    needs = [max(stage(p) for p in chunk if p[0][0] == "s") for chunk in chunks]
    return small, big, cols, groups, chunks, needs


def dense_rows(chunks):
    room = P - len(chunks[0])
    assert room < DENSE and len(chunks[-1]) + DENSE - room <= P
    return {0: (0, room), len(chunks) - 1: (room, DENSE)}


def selectors(chunks, ns, nb):
    use = []
    for c, chunk in enumerate(chunks):
        for side in (0, 1):
            for kind in "sb":
                if any(pair[side][0] == kind for pair in chunk):
                    use.append((c, side, kind))
    return use


def build(nc, rows, idx_big, ids_small, tables, big_tables, dense, w1, w2, vectors, tail_rows, ident_c, group_c, add_c,
          select_c, out):
    f32, bf16, i32 = mybir.dt.float32, mybir.dt.bfloat16, mybir.dt.int32
    ALU = mybir.AluOpType
    ACT = mybir.ActivationFunctionType
    AX = mybir.AxisListType

    small, big, cols, groups, chunks, needs = plan(rows)
    NS, NBIG, NG, NCH = len(small), len(big), len(groups), len(chunks)
    KS, KB = PARTS * NS, PARTS * NBIG
    col0 = [sum(cols[:f]) for f in range(NS + 1)]
    uses = selectors(chunks, NS, NBIG)
    with_big = [any(b[0] == "b" for _, b in chunk) for chunk in chunks]
    assert all(b - a <= HALF for _, a, b in PICKS)
    last_pick = [max(k for k, (_, a, b) in enumerate(PICKS) if a < end and b > start) for start, end in FINISH]
    assert SNAP_AFTER[-1] == NG - 1 and last_pick == sorted(last_pick)
    dense_of = dense_rows(chunks)
    V_P, V_C, V_B1 = 0, 1, 2

    with ExitStack() as ctx:
        def sb(name, shape, dt):
            return ctx.enter_context(nc.sbuf_tensor(name, shape, dt))

        def sem(name):
            return ctx.enter_context(nc.semaphore(name))

        table = sb("table", [P, col0[NS] * D], f32)
        row_sum = sb("row_sum", [P, col0[NS]], f32)
        rest = sb("rest", [P, 2, GROUP * CMAX], f32)
        parts = sb("parts", [P, NS, QUAD], bf16)
        ids_s = sb("ids_s", [P, B], i32)
        row_i = sb("row_i", [P, B], i32)
        col_i = sb("col_i", [P, B], i32)
        row_b = sb("row_b", [P, B], bf16)
        col_b = sb("col_b", [P, B], bf16)
        onehot = sb("onehot", [P, NS, B], bf16)
        col_mask = sb("col_mask", [P, NG, B], bf16)
        masked = sb("masked", [P, 2, B], bf16)
        stack_s = sb("stack_s", [KS, len(SNAP_AFTER), B], bf16)
        idx = sb("idx", [P, TILES * NBIG], i32)
        rows_b = sb("rows_b", [P, TILES, NBIG, D], f32)
        sum_b = sb("sum_b", [P, TILES, NBIG], f32)
        rest_b = sb("rest_b", [P, TILES, NBIG], f32)
        parts_b = sb("parts_b", [P, TILES, PARTS, NBIG], bf16)
        stack_b = sb("stack_b", [KB, B], bf16)
        factor = sb("factor", [P, 2, B], f32)
        z = sb("z", [P, NCH, B], f32)
        w1_s = sb("w1_s", [P, NCH, N1], f32)
        w2_s = sb("w2_s", [P, NB1, N2], f32)
        vec = sb("vec", [P, V_B1 + NB1], f32)
        tail = sb("tail", [P, 2, N2], f32)
        ident = sb("ident", [P, P], bf16)
        zeros = sb("zeros", [P, P], bf16)
        group_rows = sb("group_rows", [NS, NG * P], bf16)
        add_cols = sb("add_cols", [P, NG * KS], bf16)
        select = sb("select", [KS, len(uses) * P], bf16)
        h1 = sb("h1", [P, NB1, B], f32)
        h2 = sb("h2", [P, TILES, N2], f32)
        h2_w3 = sb("h2_w3", [P, TILES, N2], f32)
        y = sb("y", [P, TILES], f32)

        bank = [ctx.enter_context(nc.psum_tensor(f"bank{i}", [P, 2, B], f32)) for i in range(2)]
        low = [bank[0][:, 0, :], bank[0][:, 1, :], bank[1][:, 0, :], bank[1][:, 1, :]]
        high = [ctx.enter_context(nc.psum_tensor(f"bank{i}", [P, B], f32)) for i in range(4, 8)]
        PICK, STACK = high[0], high[2]
        SEL_A, SEL_B = high[1], high[3]
        SEL = (SEL_A, SEL_B)
        L2_BANKS = (PICK, STACK, SEL_A, SEL_B)
        sel_b = [x[:, :].rearrange("p (s c n) -> p s c n", s=2, c=2) for x in (SEL_A, SEL_B)]

        def adder(g):
            return add_cols[:, g * KS:(g + 1) * KS]

        def selector(c, side, kind, m):
            u = uses.index((c, side, kind))
            return select[0:KS if kind == "s" else KB, u * P:u * P + m]

        ids_in, idx_in, ident_in, vec_in, group_in = (
            sem("ids_in"), sem("idx_in"), sem("ident_in"), sem("vec_in"), sem("group_in"))
        add_in, select_in, w2_in = sem("add_in"), sem("select_in"), sem("w2_in")
        dense_in = {c: sem(f"dense_in{c}") for c in dense_of}
        w1_in = [sem(f"w1_in{c}") for c in range(NCH)]
        table_in = [[sem(f"table_in{g}_{h}") for h in (0, 1)] for g in range(NG)]
        gathered = [sem(f"gathered{t}") for t in range(TILES)]
        out_written = sem("out_written")
        parts_zeroed, zeros_made = sem("parts_zeroed"), sem("zeros_made")
        ids_cut, ids_cut_b = sem("ids_cut"), sem("ids_cut_b")
        row_spread, row_copied = sem("row_spread"), sem("row_copied")
        col_spread, col_copied = sem("col_spread"), sem("col_copied")
        onehot_made, mask_made = sem("onehot_made"), sem("mask_made")
        rows_summed, high_made, rest_made, mid_made, parts_made = (
            sem("rows_summed"), sem("high_made"), sem("rest_made"), sem("mid_made"), sem("parts_made"))
        picked, masked_made, stacked, snapped = sem("picked"), sem("masked_made"), sem("stacked"), sem("snapped")
        big_summed, big_high, big_rest, big_mid, big_parts = (
            sem("big_summed"), sem("big_high"), sem("big_rest"), sem("big_mid"), sem("big_parts"))
        big_turned, big_stacked = sem("big_turned"), sem("big_stacked")
        selected, factor_copied, z_made = sem("selected"), sem("factor_copied"), sem("z_made")
        l1_done, h1_made, l2_done, h2_made, y_made = (
            sem("l1_done"), sem("h1_made"), sem("l2_done"), sem("h2_made"), sem("y_made"))
        tail_in = sem("tail_in")

        block = ctx.enter_context(nc.Block())

        def turn_for(r):
            return next(k for k, (c, _, b) in enumerate(PICKS) if with_big[c] and b >= RANGES[r][1])

        def turned(r):
            return factors(turn_for(r))[0]

        def fields_of(g, h):
            f0, n, _ = groups[g]
            m = (n + 1) // 2
            return range(f0, f0 + m) if h == 0 else range(f0 + m, f0 + n)

        def halves(g):
            return sum(-(-n // 2) for _, n, _ in groups[:g])

        def factors(k):
            _, a, b = PICKS[k]
            return SEL[k % 2][:, 0:b - a], SEL[k % 2][:, HALF:HALF + b - a]

        @block.sync
        def _(sp):
            def load_table(g):
                for h in (0, 1):
                    for f in fields_of(g, h):
                        for q in range(PIECES[g]):
                            a, b = ((col0[f] * PIECES[g] + (q + e) * cols[f]) * D // PIECES[g] for e in (0, 1))
                            sp.dma_start(table[:, a:b], tables[:, a:b]).then_inc(table_in[g][h], 16)

            def load_w1(c):
                sp.dma_start(w1_s[:, c, :], w1[:, c, :]).then_inc(w1_in[c], 16)

            def load_dense(c):
                a, b = dense_of[c]
                m = len(chunks[c])
                sp.dma_start(z[m:m + b - a, c, :], dense[a:b, :]).then_inc(dense_in[c], 16)

            sp.dma_start(ids_s[:, :], ids_small).then_inc(ids_in, 16)
            sp.dma_start(vec[:, :], vectors).then_inc(vec_in, 16)
            load_table(0)
            for g in range(1, NG):
                load_table(g)
                if g == 1:
                    sp.dma_start(add_cols[:, :], add_c).then_inc(add_in, 16)
                if g == 3:
                    sp.dma_start(select[:, :], select_c).then_inc(select_in, 16)
                if g == 4:
                    load_w1(0)
                    load_dense(0)
                if g == 5:
                    load_w1(1)
            for c in range(2, NCH):
                load_w1(c)
            load_dense(NCH - 1)
            sp.dma_start(w2_s[:, :, :], w2).then_inc(w2_in, 16)
            sp.dma_start(tail[:, :, :], tail_rows.broadcast_to([P, 2, N2])).then_inc(tail_in, 16)
            sp.wait_ge(y_made, TILES)
            sp.dma_start(out.rearrange("(p t) one -> p (t one)", t=TILES), y[:, :]).then_inc(out_written, 16)
            sp.wait_ge(out_written, 16)

        @block.gpsimd
        def _(pool):
            pool.wait_ge(idx_in, 16)
            for t in range(TILES):
                for f in range(NBIG):
                    k = t * NBIG + f
                    nc.gpsimd.indirect_dma_start(
                        rows_b[:, t, f, :], None, big_tables[f],
                        bass.IndirectOffsetOnAxis(ap=idx[:, k:k + 1], axis=0)).then_inc(gathered[t], 16)

        @block.scalar
        def _(act):
            act.dma_start(idx[:, :], idx_big).then_inc(idx_in, 16)
            act.dma_start(ident[:, :], ident_c).then_inc(ident_in, 16)
            act.dma_start(group_rows[:, :], group_c).then_inc(group_in, 16)

            def copy_rows(g, h):
                f0, n, _ = groups[g]
                m = min(2, n - 2 * h)
                act.wait_ge(row_spread, halves(g) + h + 1)
                nc.scalar.copy(onehot[:, f0 + 2 * h:f0 + 2 * h + m, :], bank[h][:, 0:m, :]).then_inc(row_copied, 1)

            def copy_cols(g):
                q = groups[g][1] * QUAD
                act.wait_ge(col_spread, g + 1)
                nc.scalar.copy(col_mask[0:q, g, :], SEL_B[0:q, :]).then_inc(col_copied, 1)

            def snap(s):
                act.wait_ge(stacked, SNAP_AFTER[s] + 1)
                nc.scalar.copy(stack_s[:, s, :], STACK[0:KS, :]).then_inc(snapped, 1)

            def copy_factor(k):
                c, a, b = PICKS[k]
                m = len(chunks[c])
                act.wait_ge(selected, k + 1)
                if k >= 2:
                    act.wait_ge(z_made, k - 1)
                nc.scalar.copy(factor[0:m, k % 2, 0:b - a], factors(k)[0][0:m]).then_inc(factor_copied, 1)

            def sum_big(t, h):
                if h == 0:
                    act.wait_ge(gathered[t], 16 * NBIG)
                for f in range(h * NBIG // 2, (h + 1) * NBIG // 2):
                    i = nc.scalar.activation(rows_b[:, t, f, :], rows_b[:, t, f, :], ACT.Copy,
                                             accum_out=sum_b[:, t, f:f + 1])
                if h == 1:
                    i.then_inc(big_summed, 1)

            def copy_turned(r):
                a, b = RANGES[r]
                act.wait_ge(big_turned, r + 1)
                nc.scalar.copy(stack_b[:, a:b], turned(r)[0:KB, 0:b - a]).then_inc(big_stacked, 1)

            def relu1(r, n):
                a, b = FINISH[r]
                if r == 0 and n == 0:
                    act.wait_ge(vec_in, 16)
                act.wait_ge(l1_done, r * NB1 + n + 1)
                nc.scalar.activation(h1[:, n, a:b], low[n][:, a:b], ACT.Relu,
                                     bias=vec[:, V_B1 + n:V_B1 + n + 1]).then_inc(h1_made, 1)

            copy_rows(0, 0)
            copy_rows(0, 1)
            copy_cols(0)
            copy_rows(1, 0)
            copy_rows(1, 1)
            copy_cols(1)
            copy_rows(2, 0)
            copy_cols(2)
            copy_rows(2, 1)
            copy_cols(3)
            copy_rows(3, 0)
            copy_rows(3, 1)
            copy_rows(4, 0)
            copy_cols(4)
            copy_rows(4, 1)
            copy_rows(5, 0)
            copy_rows(5, 1)
            copy_rows(6, 0)
            copy_rows(6, 1)
            copy_cols(5)
            sum_big(0, 0)
            copy_cols(6)
            sum_big(0, 1)
            copy_cols(7)
            copy_rows(7, 0)
            snap(0)
            copy_factor(0)
            copy_factor(1)
            sum_big(1, 0)
            sum_big(1, 1)
            copy_turned(0)
            copy_factor(2)
            snap(1)
            for n in range(3, 6):
                copy_factor(n)
            snap(2)
            copy_factor(6)
            copy_turned(1)
            snap(3)
            copy_factor(7)
            copy_factor(8)
            copy_turned(2)
            for n in range(9, 13):
                copy_factor(n)
            for n in range(4):
                relu1(0, n)
            copy_factor(13)
            for n in range(4):
                relu1(1, n)

        @block.vector
        def _(dve):
            nc.vector.memset(zeros[:, :], 0.0).then_inc(zeros_made, 1)
            nc.vector.memset(parts[:, :, :], 0.0).then_inc(parts_zeroed, 1)
            dve.wait_ge(ids_in, 16)
            nc.vector.tensor_single_scalar(row_i[:, :], ids_s[:, :], P - 1, ALU.bitwise_and).then_inc(ids_cut, 1)
            dve.wait_ge(ids_cut, 1)
            nc.vector.tensor_copy(row_b[:, :], row_i[:, :]).then_inc(ids_cut_b, 1)
            nc.vector.tensor_single_scalar(col_i[:, :], ids_s[:, :], 7, ALU.logical_shift_right).then_inc(ids_cut, 1)
            dve.wait_ge(ids_cut, 2)
            nc.vector.tensor_copy(col_b[:, :], col_i[:, :]).then_inc(ids_cut_b, 1)
            dve.wait_ge(vec_in, 16)

            def make_onehot(g):
                f0, n, _ = groups[g]
                dve.wait_ge(row_copied, halves(g + 1))
                nc.vector.tensor_scalar(onehot[:, f0:f0 + n, :], onehot[:, f0:f0 + n, :], vec[:, V_P:V_P + 1],
                                        None, ALU.is_equal).then_inc(onehot_made, 1)

            def make_mask(g):
                q = groups[g][1] * QUAD
                dve.wait_ge(col_copied, g + 1)
                nc.vector.tensor_scalar(col_mask[0:q, g, :], col_mask[0:q, g, :], vec[0:q, V_C:V_C + 1],
                                        None, ALU.is_equal).then_inc(mask_made, 1)

            def sum_rows(g, h):
                fields = fields_of(g, h)
                a, b = col0[fields[0]], col0[fields[-1] + 1]
                dve.wait_ge(table_in[g][h], 16 * PIECES[g] * len(fields))
                src = table[:, a * D:b * D].rearrange("p (r d) -> p r d", d=D)
                nc.vector.tensor_reduce(row_sum[:, a:b], src, AX.X, ALU.add).then_inc(rows_summed, 1)

            def split_sums(g, step):
                f0, n, c = groups[g]
                s = row_sum[:, col0[f0]:col0[f0 + n]].rearrange("p (f c) -> p f c", c=c)
                part = [parts[:, f0:f0 + n, k * CMAX:k * CMAX + c] for k in range(PARTS)]
                r = rest[:, g % 2, 0:n * c].rearrange("p (f c) -> p f c", c=c)
                if step == 0:
                    dve.wait_ge(rows_summed, 2 * g + 2)
                    if g == 0:
                        dve.wait_ge(parts_zeroed, 1)
                    nc.vector.tensor_copy(part[0], s).then_inc(high_made, 1)
                elif step == 1:
                    dve.wait_ge(high_made, g + 1)
                    nc.vector.tensor_tensor(r, s, part[0], ALU.subtract).then_inc(rest_made, 1)
                elif step == 2:
                    dve.wait_ge(rest_made, g + 1)
                    nc.vector.tensor_copy(part[1], r).then_inc(mid_made, 1)
                else:
                    dve.wait_ge(mid_made, g + 1)
                    nc.vector.tensor_tensor(part[2], r, part[1], ALU.subtract).then_inc(parts_made, 1)

            def mask_picked(g):
                q = groups[g][1] * QUAD
                dve.wait_ge(mask_made, g + 1)
                dve.wait_ge(picked, g + 1)
                if g >= 2:
                    dve.wait_ge(stacked, g - 1)
                nc.vector.tensor_tensor(masked[0:q, g % 2, :], PICK[0:q, :], col_mask[0:q, g, :],
                                        ALU.mult).then_inc(masked_made, 1)

            def multiply(k):
                c, a, b = PICKS[k]
                m = len(chunks[c])
                dve.wait_ge(factor_copied, k + 1)
                nc.vector.tensor_tensor(z[0:m, c, a:b], factor[0:m, k % 2, 0:b - a], factors(k)[1][0:m],
                                        ALU.mult).then_inc(z_made, 1)

            def sum_big(t):
                dve.wait_ge(gathered[t], 16 * NBIG)
                nc.vector.tensor_reduce(sum_b[:, t, :], rows_b[:, t, :, :], AX.X, ALU.add).then_inc(big_summed, 1)

            def split_big(r, step):
                a, b = (x // P for x in RANGES[r])
                s, high, mid = sum_b[:, a:b, :], parts_b[:, a:b, 0, :], parts_b[:, a:b, 1, :]
                rest = rest_b[:, a:b, :]
                if step == 0:
                    dve.wait_ge(big_summed, b)
                    nc.vector.tensor_copy(high, s).then_inc(big_high, 1)
                elif step == 1:
                    dve.wait_ge(big_high, r + 1)
                    nc.vector.tensor_tensor(rest, s, high, ALU.subtract).then_inc(big_rest, 1)
                elif step == 2:
                    dve.wait_ge(big_rest, r + 1)
                    nc.vector.tensor_copy(mid, rest).then_inc(big_mid, 1)
                else:
                    dve.wait_ge(big_mid, r + 1)
                    nc.vector.tensor_tensor(parts_b[:, a:b, 2, :], rest, mid, ALU.subtract).then_inc(big_parts, 1)

            def finish(t):
                if t == 0:
                    dve.wait_ge(tail_in, 16)
                dve.wait_ge(l2_done, t + 1)
                nc.vector.tensor_tensor(h2[:, t, :], L2_BANKS[t][:, 0:N2], tail[:, 0, :], ALU.add).then_inc(h2_made, 1)
                dve.wait_ge(h2_made, t + 1)
                nc.vector.scalar_tensor_tensor(h2_w3[:, t, :], h2[:, t, :], 0.0, tail[:, 1, :], ALU.max, ALU.mult,
                                               accum_out=y[:, t:t + 1]).then_inc(y_made, 1)

            sum_rows(0, 0)
            make_onehot(0)
            make_mask(0)
            sum_rows(0, 1)
            split_sums(0, 0)
            sum_rows(1, 0)
            split_sums(0, 1)
            make_onehot(1)
            split_sums(0, 2)
            sum_rows(1, 1)
            split_sums(0, 3)
            make_mask(1)
            split_sums(1, 0)
            make_mask(2)
            split_sums(1, 1)
            make_mask(3)
            mask_picked(0)
            sum_rows(2, 0)
            split_sums(1, 2)
            sum_rows(2, 1)
            split_sums(1, 3)
            make_onehot(2)
            split_sums(2, 0)
            sum_rows(3, 0)
            split_sums(2, 1)
            mask_picked(1)
            split_sums(2, 2)
            sum_rows(3, 1)
            split_sums(2, 3)
            make_mask(4)
            split_sums(3, 0)
            make_mask(5)
            split_sums(3, 1)
            mask_picked(2)
            split_sums(3, 2)
            make_mask(6)
            split_sums(3, 3)
            make_onehot(3)
            sum_rows(4, 0)
            mask_picked(3)
            make_onehot(4)
            sum_rows(4, 1)
            multiply(0)
            split_sums(4, 0)
            multiply(1)
            split_sums(4, 1)
            sum_rows(5, 0)
            split_sums(4, 2)
            make_mask(7)
            split_sums(4, 3)
            sum_rows(5, 1)
            split_big(0, 0)
            split_sums(5, 0)
            split_big(0, 1)
            split_big(0, 2)
            split_sums(5, 1)
            split_big(0, 3)
            split_sums(5, 2)
            split_sums(5, 3)
            make_onehot(5)
            mask_picked(4)
            multiply(2)
            mask_picked(5)
            sum_rows(6, 0)
            sum_rows(6, 1)
            multiply(3)
            split_sums(6, 0)
            multiply(4)
            split_sums(6, 1)
            make_onehot(6)
            multiply(5)
            split_sums(6, 2)
            make_onehot(7)
            split_sums(6, 3)
            sum_rows(7, 0)
            sum_rows(7, 1)
            mask_picked(6)
            for n in range(3):
                split_sums(7, n)
            sum_big(2)
            split_sums(7, 3)
            for n in range(4):
                split_big(1, n)
            mask_picked(7)
            multiply(6)
            sum_big(3)
            for n in range(3):
                split_big(2, n)
            multiply(7)
            split_big(2, 3)
            for n in range(8, 14):
                multiply(n)
            for n in range(4):
                finish(n)

        @block.tensor
        def _(pe):
            def spread_rows(g, h):
                f0, n, _ = groups[g]
                if g >= 1:
                    pe.wait_ge(row_copied, halves(g - 1) + min(h + 1, halves(g) - halves(g - 1)))
                for j in range(2 * h, min(2 * h + 2, n)):
                    i = nc.tensor.matmul(low[j], ident[:, f0 + j:f0 + j + 1].broadcast_to([P, P]), row_b[:, :],
                                         start=True, stop=True)
                i.then_inc(row_spread, 1)

            def spread_cols(g):
                q = groups[g][1] * QUAD
                if g == 0:
                    pe.wait_ge(group_in, 16)
                    pe.wait_ge(ids_cut_b, 2)
                else:
                    pe.wait_ge(col_copied, g)
                nc.tensor.matmul(SEL_B[0:q, :], group_rows[:, g * P:g * P + q],
                                 col_b[0:NS, :], start=True, stop=True).then_inc(col_spread, 1)

            def keep_clock(stage, n):
                for _ in range(n):
                    if stage == 0:
                        nc.tensor.matmul(SEL_A[:, :], ident[:, :], row_b[:, :], start=True, stop=True)
                    elif stage == 1:
                        pe.wait_ge(row_copied, halves(NG))
                        nc.tensor.matmul(low[NB1 - 1], ident[:, :], row_b[:, :], start=True, stop=True)
                    else:
                        nc.tensor.matmul(low[NB1 - 1], zeros[:, :], row_b[:, :], start=False, stop=False,
                                         skip_group_check=True)

            def pick(g):
                f0, n, _ = groups[g]
                pe.wait_ge(onehot_made, g + 1)
                pe.wait_ge(parts_made, g + 1)
                if g >= 1:
                    pe.wait_ge(masked_made, g)
                for j in range(n):
                    i = nc.tensor.matmul(PICK[j * QUAD:(j + 1) * QUAD, :], parts[:, f0 + j, :], onehot[:, f0 + j, :],
                                         start=True, stop=True)
                i.then_inc(picked, 1)

            def stack(g):
                q = groups[g][1] * QUAD
                if g == 0:
                    pe.wait_ge(add_in, 16)
                pe.wait_ge(masked_made, g + 1)
                done = sum(1 for last in SNAP_AFTER if last < g)
                if done:
                    pe.wait_ge(snapped, done)
                nc.tensor.matmul(STACK[0:KS, :], adder(g)[0:q, :], masked[0:q, g % 2, :],
                                 start=g == 0, stop=g == NG - 1, skip_group_check=True).then_inc(stacked, 1)

            def select_pairs(k):
                c, a, b = PICKS[k]
                m, s = len(chunks[c]), needs[c]
                pe.wait_ge(snapped, s + 1)
                if with_big[c]:
                    pe.wait_ge(big_stacked, sum(1 for _, end in RANGES if end <= b))
                if k == 0:
                    pe.wait_ge(select_in, 16)
                elif k == 1:
                    pe.wait_ge(col_copied, NG)
                else:
                    pe.wait_ge(z_made, k - 1)
                for side, to in enumerate(factors(k)):
                    mine = [kind for kind in "sb" if (c, side, kind) in uses]
                    for kind in mine:
                        src = stack_s[:, s, a:b] if kind == "s" else stack_b[:, a:b]
                        i = nc.tensor.matmul(to[0:m], selector(c, side, kind, m), src,
                                             start=kind == mine[0], stop=kind == mine[-1])
                i.then_inc(selected, 1)

            def turn_big(r):
                a, b = RANGES[r]
                pe.wait_ge(big_parts, r + 1)
                pe.wait_ge(z_made, turn_for(r) - 1)
                for t in range(a // P, b // P):
                    i = nc.tensor.matmul(turned(r)[0:KB, t * P - a:(t + 1) * P - a], parts_b[:, t, :, :], ident[:, :],
                                         start=True, stop=True)
                i.then_inc(big_turned, 1)

            def layer1(k, h):
                c, a, b = PICKS[k]
                if k == 0:
                    pe.wait_ge(row_copied, halves(NG))
                if c in dense_of:
                    pe.wait_ge(dense_in[c], 16)
                pe.wait_ge(w1_in[c], 16)
                pe.wait_ge(z_made, k + 1)
                a_dense, b_dense = dense_of.get(c, (0, 0))
                rows_c = len(chunks[c]) + b_dense - a_dense
                done = sum(1 for last in last_pick if last < k)
                for n in (2 * h, 2 * h + 1):
                    if done:
                        pe.wait_ge(h1_made, (done - 1) * NB1 + n + 1)
                    w = nc.tensor.matmul(low[n][:, a:b], w1_s[0:rows_c, c, n * P:(n + 1) * P], z[0:rows_c, c, a:b],
                                         start=k == 0, stop=k in last_pick, skip_group_check=True)
                    if k in last_pick:
                        w.then_inc(l1_done, 1)

            def layer2(t):
                if t == 0:
                    pe.wait_ge(w2_in, 16)
                    pe.wait_ge(masked_made, NG)
                if t == 1:
                    pe.wait_ge(snapped, len(SNAP_AFTER))
                if t == 2:
                    pe.wait_ge(z_made, len(PICKS))
                r = next(r for r, (_, end) in enumerate(FINISH) if t * P < end)
                for n in range(NB1):
                    pe.wait_ge(h1_made, r * NB1 + n + 1)
                    w = nc.tensor.matmul(L2_BANKS[t][:, 0:N2], h1[:, n, t * P:(t + 1) * P], w2_s[:, n, :],
                                         start=n == 0, stop=n == NB1 - 1)
                w.then_inc(l2_done, 1)

            pe.wait_ge(ident_in, 16)
            pe.wait_ge(zeros_made, 1)
            pe.wait_ge(ids_cut_b, 1)
            spread_rows(0, 0)
            spread_rows(0, 1)
            spread_cols(0)
            spread_rows(1, 0)
            spread_rows(1, 1)
            spread_cols(1)
            spread_rows(2, 0)
            spread_rows(2, 1)
            spread_cols(2)
            spread_rows(3, 0)
            spread_cols(3)
            spread_rows(3, 1)
            spread_cols(4)
            pick(0)
            spread_rows(4, 0)
            spread_rows(4, 1)
            stack(0)
            spread_rows(5, 0)
            spread_cols(5)
            keep_clock(0, 2)
            spread_rows(5, 1)
            keep_clock(0, 1)
            pick(1)
            spread_rows(6, 0)
            spread_rows(6, 1)
            keep_clock(0, 2)
            spread_rows(7, 0)
            keep_clock(0, 1)
            stack(1)
            spread_cols(6)
            keep_clock(0, 4)
            pick(2)
            spread_cols(7)
            keep_clock(0, 3)
            stack(2)
            keep_clock(0, 3)
            pick(3)
            keep_clock(0, 7)
            stack(3)
            keep_clock(0, 3)
            select_pairs(0)
            select_pairs(1)
            keep_clock(1, 3)
            layer1(0, 0)
            layer1(0, 1)
            layer1(1, 0)
            layer1(1, 1)
            pick(4)
            keep_clock(2, 3)
            turn_big(0)
            keep_clock(2, 2)
            select_pairs(2)
            keep_clock(2, 2)
            pick(5)
            stack(4)
            layer1(2, 0)
            stack(5)
            layer1(2, 1)
            select_pairs(3)
            select_pairs(4)
            keep_clock(2, 2)
            select_pairs(5)
            layer1(3, 0)
            layer1(3, 1)
            pick(6)
            layer1(4, 0)
            layer1(4, 1)
            stack(6)
            layer1(5, 0)
            pick(7)
            select_pairs(6)
            layer1(5, 1)
            stack(7)
            turn_big(1)
            layer1(6, 0)
            select_pairs(7)
            select_pairs(8)
            layer1(6, 1)
            turn_big(2)
            layer1(7, 0)
            layer1(7, 1)
            select_pairs(9)
            layer1(8, 0)
            layer1(8, 1)
            select_pairs(10)
            layer1(9, 0)
            layer1(9, 1)
            select_pairs(11)
            select_pairs(12)
            layer1(10, 0)
            layer1(10, 1)
            layer1(11, 0)
            layer1(11, 1)
            select_pairs(13)
            layer1(12, 0)
            layer1(12, 1)
            layer1(13, 0)
            layer1(13, 1)
            for n in range(4):
                layer2(n)


def kernel(**inputs):
    import ml_dtypes
    import concourse.bacc as bacc
    from concourse.bass_utils import run_bass_kernel_spmd

    x = {k: np.asarray(v) for k, v in inputs.items()}
    tbl = [x[f"tbl_{f}"] for f in range(FIELDS)]
    rows = [t.shape[0] for t in tbl]
    small, big, cols, groups, chunks, _ = plan(rows)
    NS, NBIG = len(small), len(big)
    KS, KB = PARTS * NS, PARTS * NBIG

    padded = []
    for f, c in zip(small, cols):
        t = np.concatenate([tbl[f], np.zeros((c * P - rows[f], D), tbl[f].dtype)])
        padded.append(t.reshape(c, P, D).transpose(1, 0, 2).reshape(P, c * D))
    tables = np.concatenate(padded, axis=1)
    order = np.arange(B).reshape(P, TILES).T.reshape(B)
    ids = x["ids"][order]
    ids_small = np.zeros((P // QUAD, QUAD, B), ids.dtype)
    ids_small[:, :NS] = ids[:, small].T
    ids_small = ids_small.reshape(P, B)
    idx_big = np.ascontiguousarray(ids[:, big].reshape(TILES, P, NBIG).transpose(1, 0, 2).reshape(P, TILES * NBIG))

    upper = {pair: k for k, pair in enumerate(zip(*np.triu_indices(FIELDS, k=1)))}
    field = {("s", i): f for i, f in enumerate(small)}
    field.update({("b", i): f for i, f in enumerate(big)})
    W = x["W_top1"]
    w1 = np.zeros((P, len(chunks), N1), W.dtype)
    for c, chunk in enumerate(chunks):
        at = [upper[tuple(sorted((field[a], field[b])))] for a, b in chunk]
        w1[:len(at), c] = W[at]
    for c, (a, b) in dense_rows(chunks).items():
        w1[len(chunks[c]):len(chunks[c]) + b - a, c] = W[W.shape[0] - DENSE:][a:b]
    w2 = np.ascontiguousarray(x["W_top2"].reshape(NB1, P, N2).transpose(1, 0, 2))

    slot = np.arange(P) % QUAD
    column = np.where(slot < PARTS * CMAX, slot % CMAX, -1)
    vectors = np.concatenate([
        np.arange(P, dtype=np.float32)[:, None], column.astype(np.float32)[:, None],
        x["b_top1"].reshape(NB1, P).T], axis=1)
    tail_rows = np.stack([x["b_top2"].reshape(N2), x["W_top3"].reshape(N2)])[None]
    ident = np.eye(P, dtype=ml_dtypes.bfloat16)
    group_rows = np.zeros((NS, len(groups) * P), ml_dtypes.bfloat16)
    for g, (f0, n, _) in enumerate(groups):
        for j in range(n):
            group_rows[f0 + j, g * P + j * QUAD:g * P + (j + 1) * QUAD] = 1
    uses = selectors(chunks, NS, NBIG)
    add_cols = np.zeros((P, len(groups) * KS), ml_dtypes.bfloat16)
    for g, (f0, n, _) in enumerate(groups):
        for j in range(n):
            for q in range(PARTS * CMAX):
                add_cols[j * QUAD + q, g * KS + q // CMAX * NS + f0 + j] = 1
    select = np.zeros((KS, len(uses) * P), ml_dtypes.bfloat16)
    for u, (c, side, kind) in enumerate(uses):
        for m, pair in enumerate(chunks[c]):
            if pair[side][0] == kind:
                for k in range(PARTS):
                    select[k * (NS if kind == "s" else NBIG) + pair[side][1], u * P + m] = 1

    nc = bacc.Bacc("TRN2", target_bir_lowering=False, num_devices=1)
    arrays = {
        "idx_big": idx_big, "ids_small": ids_small, "small_tables": tables,
        "dense": np.ascontiguousarray(x["dense_ctx"][order].T), "w1": w1, "w2": w2, "vectors": vectors, "tail_rows": tail_rows,
        "ident": ident, "group_rows": group_rows, "add_cols": add_cols, "select": select,
    }
    for f in big:
        arrays[f"big_table_{f}"] = tbl[f]
    ap = {n: nc.dram_tensor("in_" + n, a.shape, mybir.dt.from_np(a.dtype), kind="ExternalInput").ap() for n, a in arrays.items()}
    out = nc.dram_tensor("y_out", (B, 1), mybir.dt.float32, kind="ExternalOutput").ap()
    build(nc, rows, ap["idx_big"], ap["ids_small"], ap["small_tables"], [ap[f"big_table_{f}"] for f in big],
          ap["dense"], ap["w1"], ap["w2"], ap["vectors"], ap["tail_rows"], ap["ident"], ap["group_rows"], ap["add_cols"], ap["select"], out)
    r = run_bass_kernel_spmd(nc, [{"in_" + n: a for n, a in arrays.items()}], core_ids=[0])
    return r.results[0]["y_out"]
```
